# Optimizing a Trainium2 kernel written in Bass

```python
import numpy as np
import jax
import jax.numpy as jnp

def _softmax(x, axis=-1):
    return jax.nn.softmax(x, axis=axis)

def _gelu(x):
    return jax.nn.gelu(x, approximate=True)

def _silu(x):
    return jax.nn.silu(x)

def _sigmoid(x):
    return jax.nn.sigmoid(x)

def _layernorm(x, axis=-1, eps=1e-05):
    m = jnp.mean(x, axis=axis, keepdims=True)
    v = jnp.var(x, axis=axis, keepdims=True)
    return (x - m) / jnp.sqrt(v + eps)

def _scatter_add(tgt, idx, src, axis=0):
    return tgt.at[idx].add(src)

def _segment_sum(src, seg, n):
    return jax.ops.segment_sum(src, seg, n)
kernel_name = 'mk_seq_postln_d1_jaxref_r4_c9e7ab'

def setup_inputs(seed: int=0):
    np.random.seed(seed)
    _w = jnp.asarray

    def _L0_attn_setup():
        import jax, jax.numpy as jnp
        import numpy as np
        B, T, D_MODEL, D_STATE = (8, 512, 256, 64)
        key = jax.random.key(seed)
        ks = jax.random.split(key, 11)

        def lecun(k, shape):
            fan_in = shape[0]
            return jax.random.normal(k, shape, jnp.float32) / jnp.sqrt(jnp.float32(fan_in))
        return {'x': jax.random.normal(ks[0], (B, T, D_MODEL), jnp.float32), 'W_in': lecun(ks[1], (D_MODEL, D_STATE)), 'b_in': jnp.zeros((D_STATE,), jnp.float32), 'W_gate': lecun(ks[2], (D_MODEL, D_MODEL)), 'b_gate': jnp.zeros((D_MODEL,), jnp.float32), 'A': lecun(ks[3], (D_STATE, D_STATE)), 'Bm': lecun(ks[4], (D_STATE, D_STATE)), 'C': lecun(ks[5], (D_MODEL, D_STATE)), 'D': lecun(ks[6], (D_MODEL, D_STATE)), 'W_out': lecun(ks[7], (D_MODEL, D_MODEL)), 'b_out': jnp.zeros((D_MODEL,), jnp.float32)}
    _L0_attn_in = _L0_attn_setup()

    def _L0_ffn_setup():
        import jax, jax.numpy as jnp
        import numpy as np

        def _binarize(w):
            alpha = jax.lax.stop_gradient(jnp.mean(jnp.abs(w), axis=1, keepdims=True))
            bw = alpha * jnp.sign(w)
            return w + jax.lax.stop_gradient(bw - w)
        key = jax.random.key(seed)
        k1, k2, k3, k4, k5 = jax.random.split(key, 5)
        D, H = (256, 1024)
        x = jax.random.normal(k1, (64, 196, D), dtype=jnp.float32)
        w1 = jax.random.normal(k2, (H, D), dtype=jnp.float32) * 0.02
        b1 = jax.random.normal(k3, (H,), dtype=jnp.float32) * 0.02
        w2 = jax.random.normal(k4, (D, H), dtype=jnp.float32) * 0.02
        b2 = jax.random.normal(k5, (D,), dtype=jnp.float32) * 0.02
        return {'x': x, 'w1': w1, 'b1': b1, 'w2': w2, 'b2': b2}
    _L0_ffn_in = _L0_ffn_setup()
    _d = {'L0_attn_x': _L0_attn_in['x'], 'L0_attn_W_in': _L0_attn_in['W_in'], 'L0_attn_b_in': _L0_attn_in['b_in'], 'L0_attn_W_gate': _L0_attn_in['W_gate'], 'L0_attn_b_gate': _L0_attn_in['b_gate'], 'L0_attn_A': _L0_attn_in['A'], 'L0_attn_Bm': _L0_attn_in['Bm'], 'L0_attn_C': _L0_attn_in['C'], 'L0_attn_D': _L0_attn_in['D'], 'L0_attn_W_out': _L0_attn_in['W_out'], 'L0_attn_b_out': _L0_attn_in['b_out'], 'L0_ffn_w1': _L0_ffn_in['w1'], 'L0_ffn_b1': _L0_ffn_in['b1'], 'L0_ffn_w2': _L0_ffn_in['w2'], 'L0_ffn_b2': _L0_ffn_in['b2']}
    _x0 = _d['L0_attn_x']
    _d['L0_attn_x'] = jax.random.normal(jax.random.fold_in(jax.random.key(seed), 1), (2, 4096, 256), dtype=_x0.dtype)
    del _x0
    return _d

def reference(L0_attn_x, L0_attn_W_in, L0_attn_b_in, L0_attn_W_gate, L0_attn_b_gate, L0_attn_A, L0_attn_Bm, L0_attn_C, L0_attn_D, L0_attn_W_out, L0_attn_b_out, L0_ffn_w1, L0_ffn_b1, L0_ffn_w2, L0_ffn_b2):

    def _L0_attn_ref(x, W_in, b_in, W_gate, b_gate, A, Bm, C, D, W_out, b_out):
        import jax, jax.numpy as jnp
        import numpy as np
        B, T, D_MODEL, D_STATE = (8, 512, 256, 64)
        b, t, d_model = x.shape
        d_state = A.shape[0]
        u = x @ W_in + b_in
        g = jax.nn.sigmoid(x @ W_gate + b_gate)
        u_seq = jnp.swapaxes(u, 0, 1)
        g_seq = jnp.swapaxes(g, 0, 1)
        x_seq = jnp.swapaxes(x, 0, 1)

        def step(h_prev, inputs):
            u_t, g_t, x_t = inputs
            h_t = jnp.tanh(h_prev @ A + u_t @ Bm)
            y_t = h_t @ C.T + u_t @ D.T
            y_t = g_t * y_t + (1.0 - g_t) * x_t
            return (h_t, y_t)
        h0 = jnp.zeros((b, d_state), x.dtype)
        _, ys = jax.lax.scan(step, h0, xs=(u_seq, g_seq, x_seq))
        ys = jnp.swapaxes(ys, 0, 1)
        return ys @ W_out + b_out + x

    def _L0_ffn_ref(x, w1, b1, w2, b2):
        import jax, jax.numpy as jnp
        import numpy as np

        def _binarize(w):
            alpha = jax.lax.stop_gradient(jnp.mean(jnp.abs(w), axis=1, keepdims=True))
            bw = alpha * jnp.sign(w)
            return w + jax.lax.stop_gradient(bw - w)
        bw1 = _binarize(w1)
        h = jnp.einsum('bsd,hd->bsh', x, bw1) + b1
        h = jax.nn.gelu(h, approximate=False)
        bw2 = _binarize(w2)
        out = jnp.einsum('bsh,dh->bsd', h, bw2) + b2
        return out
    x = L0_attn_x
    x = _layernorm(x + _L0_attn_ref(x, L0_attn_W_in, L0_attn_b_in, L0_attn_W_gate, L0_attn_b_gate, L0_attn_A, L0_attn_Bm, L0_attn_C, L0_attn_D, L0_attn_W_out, L0_attn_b_out), axis=-1)
    x = _layernorm(x + _L0_ffn_ref(x, L0_ffn_w1, L0_ffn_b1, L0_ffn_w2, L0_ffn_b2), axis=-1)
    return x

_drawn_inputs = setup_inputs


def setup_inputs(seed=0):
    import zlib

    import numpy as np

    out = dict(_drawn_inputs(seed))
    spreads = {'L0_attn_b_in': (0.0, 0.52), 'L0_attn_b_gate': (0.0, 0.727), 'L0_attn_b_out': (0.0, 0.1)}
    factors = {'L0_ffn_b1': 8.0, 'L0_ffn_b2': 2.923}
    for name, (base, spread) in spreads.items():
        noise = np.random.default_rng([zlib.crc32(name.encode()), seed]).standard_normal(out[name].shape)
        drawn = base * np.exp(spread * noise) if base else spread * noise
        out[name] = jnp.asarray(drawn.astype(out[name].dtype))
    for name, factor in factors.items():
        out[name] = (out[name] * factor).astype(out[name].dtype)
    return out
```

```python
from contextlib import ExitStack

import concourse.bass as bass
from concourse import mybir

F32 = mybir.dt.float32
F16 = mybir.dt.float16
I32 = mybir.dt.int32
ALU = mybir.AluOpType
ACT = mybir.ActivationFunctionType
AX = mybir.AxisListType

P = 128
STEPS = 4
RING = 5
LN_EPS = 1e-5
GUESS_TOLERANCE = 2.0 ** -18
X_SCALE = 1024.0
TOP = 2.0 ** 14
EXPONENT_BITS = 0x7F800000


def gated_rnn_ffn(nc, x, W_in, b_in, W_gate, b_gate, A, Bm, C, D, W_out, b_out, w1, b1, w2, b2, out):
    BATCH, T, DM = x.shape
    NS = A.shape[0]
    H = w1.shape[0]
    KD = DM // P
    HC = H // P
    CHUNKS = P // BATCH
    L = T // CHUNKS
    NB = L // STEPS
    N = STEPS * P
    assert NS == 64 and KD == 2 and L % STEPS == 0 and (NB - 1) % RING == 0 and N == 512 and HC == 8

    x_rows = x.rearrange("b (c s) d -> (b c) s d", s=L)
    out_rows = out.rearrange("b (c s) d -> (b c) s d", s=L)

    with ExitStack() as ctx:
        def sb(name, shape, dt=F32):
            return ctx.enter_context(nc.sbuf_tensor(name, shape, dt))

        def sem(name):
            return ctx.enter_context(nc.semaphore(name))

        xT = sb("xT", [P, NB, KD, N])
        gT = sb("gT", [P, NB, KD, N])
        hu = sb("hu", [P, L + 1, P])
        w_in = sb("w_in", [P, KD, P])
        w_gate = sb("w_gate", [P, KD, DM])
        w_out = sb("w_out", [P, KD, DM])
        w_rec = sb("w_rec", [P, NS])
        cd_t = sb("cd_t", [P, DM])
        w1s = sb("w1s", [P, KD, H], F16)
        w2s = sb("w2s", [P, HC, DM], F16)
        b_in_col = sb("b_in_col", [P, 1])
        b_gate_col = sb("b_gate_col", [P, KD])
        b1_col = sb("b1_col", [P, HC])
        alpha1 = sb("alpha1", [P, HC])
        alpha2 = sb("alpha2", [P, KD])
        alpha2_row = sb("alpha2_row", [P, DM])
        half_b_out = sb("half_b_out", [P, DM])
        b2_row = sb("b2_row", [P, DM])
        ident = sb("ident", [P, P])
        ident16 = sb("ident16", [P, P], F16)
        ones = sb("ones", [P, P])
        small = sb("small", [P, 32])
        neg_half = sb("neg_half", [P, STEPS])
        flag_i = sb("flag_i", [1, 1], I32)
        ysT = sb("ysT", [P, KD, N])
        x_load = sb("x_load", [P, STEPS, DM])
        x1_rows = sb("x1_rows", [P, STEPS, DM])
        hid = sb("hid", [P, 4, 2, N], F16)
        fin = sb("fin", [P, STEPS, DM])
        stats = sb("stats", [P, 2, STEPS, 6])
        moments = sb("moments", [P, 2, STEPS, 2])
        rstd = sb("rstd", [P, 2, STEPS])

        bank = [ctx.enter_context(nc.psum_tensor(f"bank{i}", [P, N], F32)) for i in range(8)]

        s_wa = sem("first_weights_in")
        s_wb = sem("gate_weights_in")
        s_wc = sem("late_weights_in")
        s_w12 = sem("ffn_weights_in")
        s_xin = [sem(f"x_block_in{i}") for i in range(RING)]
        s_const = sem("constants_ready")
        s_ident = sem("identity_steps")
        s_half = sem("exponent_ready")
        s_h0 = sem("initial_state_ready")
        s_xt = sem("x_transposed")
        s_xtr = sem("xT_ready")
        s_umm = sem("u_product")
        s_u = sem("u_ready")
        s_scan = sem("scan_product")
        s_h = sem("state_ready")
        s_guess = sem("guess_set")
        s_gmm = sem("gate_product")
        s_g = sem("gate_ready")
        s_gx = sem("gated_x_ready")
        s_cmp = sem("compare_steps")
        s_cnt = sem("mismatches_counted")
        s_flag = sem("flag_ready")
        s_rscan = sem("repair_product")
        s_rh = sem("repair_state")
        s_done = sem("states_final")
        s_prep = sem("prep_chain")
        s_sgn = sem("signs_ready")
        s_cdp = sem("cd_transposed")
        s_cd = sem("cd_ready")
        s_wtp = sem("signs_transposed")
        s_wt = sem("sign_weights_ready")
        s_mt = sem("bound_transposed")
        s_m1 = sem("bound_reduced")
        s_mb = sem("bound_broadcast")
        s_a2p = sem("alpha2_broadcast")
        s_dg = sem("alpha2_diagonal")
        s_scale = sem("scales_ready")
        s_hb = sem("half_bias_ready")
        s_shift = sem("states_aligned")
        s_ymm = sem("y_product")
        s_t = sem("gated_y_ready")
        s_ys = sem("ys_ready")
        s_omm = sem("out_product")
        s_xl = sem("x_reloaded")
        s_xb = sem("x_plus_bias_ready")
        s_ln = sem("norm_chain")
        s_v1 = sem("first_variance_ready")
        s_rs1 = sem("first_rstd_ready")
        s_v2 = sem("second_variance_ready")
        s_rs2 = sem("second_rstd_ready")
        s_x1 = sem("x1_ready")
        s_x1t = sem("x1_transposed")
        s_xhi = sem("x1_hi_ready")
        s_xlo = sem("x1_lo_ready")
        s_x1b = sem("residual_ready")
        s_f1 = sem("hidden_product")
        s_gelu = sem("gelu_ready")
        s_hhi = sem("hidden_hi_ready")
        s_hlo = sem("hidden_lo_ready")
        s_f2 = sem("ffn_product")
        s_fin = sem("ffn_sum_ready")
        s_r2 = sem("ffn_residual_ready")
        s_or = sem("out_ready")
        s_st = sem("out_stored")

        def xrow_buf(slot):
            return gT[:, slot].rearrange("p k n -> p (k n)").rearrange("p (s d) -> p s d", d=DM)

        def rows_of(buf, n):
            return buf[:, n].rearrange("p k n -> p (k n)").rearrange("p (s d) -> p s d", d=DM)

        x1T = xT[:, :, :, :].rearrange("p b k n -> p b (k n)").bitcast(F16).rearrange(
            "p b (h s k r) -> p b h s k r", h=2, s=STEPS, k=KD)
        STAGED = 4
        w1_stage = gT[:, NB - 2:NB].rearrange("p b k n -> p (b k n)").rearrange("p (j d) -> p j d", d=DM)
        w2_stage = gT[:, NB - STAGED:NB - 2].rearrange("p b k n -> p (b k n)").rearrange("p (k h) -> p k h", k=KD)
        w1_sgn = hid[:, 0:2].rearrange("p a b n -> p (a b n)").rearrange("p (j d) -> p j d", d=DM)
        w2_sgn = hid[:, 2:4].rearrange("p a b n -> p (a b n)").rearrange("p (k h) -> p k h", k=KD)
        neg_w1 = ysT[:, :, :].rearrange("p k n -> p (k n)").bitcast(F16).rearrange("p (j d) -> p j d", d=DM)
        neg_w2 = fin[:, :, :].rearrange("p a b -> p (a b)").bitcast(F16).rearrange("p (k h) -> p k h", k=KD)
        cd_stage = x1_rows[:, 0:1, :].rearrange("p a (k n) -> p (a k) n", k=KD)
        diag = x1_rows[:, 1:2, :].rearrange("p a (k n) -> p (a k) n", k=KD)
        end_state = hu[0:NS, L, :].rearrange("p (b c) -> p b c", b=BATCH)[:, :, 0:CHUNKS - 1]
        guess = hu[0:NS, 0, :].rearrange("p (b c) -> p b c", b=BATCH)[:, :, 1:CHUNKS]
        gap = x_load[0:NS, 0, 0:P - BATCH].rearrange("p (b c) -> p b c", b=BATCH)
        gap_max = small[0:NS, 0:1]
        gap_flag = small[0:NS, 1:2]
        bound = small[:, 2:2 + HC]
        bound_max = small[:, 10:11]
        bound_all = small[0:1, 11:12]
        inv_scale = small[:, 12:13]
        hid_scale = small[:, 13:14]
        bound_pow = small[:, 14:15]
        abs_b1 = small[:, 16:16 + HC]

        def apart(eng):
            eng.wait_ge(s_const, 3)

        block = ctx.enter_context(nc.Block())

        @block.sync
        def _(sp):
            for j in range(RING):
                sp.dma_start(xrow_buf(j), x_rows[:, j * STEPS:(j + 1) * STEPS, :]).then_inc(s_xin[j], 16)
            with sp.Fori(0, (NB - 1) // RING - 1) as i:
                for q in range(RING):
                    sp.wait_ge(s_xt, i * (RING * STEPS) + (q + 1) * STEPS)
                    sp.dma_start(xrow_buf(q), x_rows[:, bass.ds(i * (RING * STEPS) + (RING + q) * STEPS, STEPS), :]
                                 ).then_inc(s_xin[q], 16)
            sp.wait_ge(s_xt, (NB - RING) * STEPS)
            sp.dma_start(xrow_buf(0), x_rows[:, L - STEPS:L, :]).then_inc(s_xin[0], 16)
            sp.wait_ge(s_xt, L - 2 * STEPS)
            sp.dma_start(w1_stage, w1.rearrange("(p j) d -> p j d", j=HC)).then_inc(s_w12, 16)
            sp.dma_start(w2_stage, w2.rearrange("(k p) h -> p k h", p=P)).then_inc(s_w12, 16)
            sp.wait_ge(s_done, 1)
            sp.dma_start(x_load[:, :, :], x_rows[:, 0:STEPS, :]).then_inc(s_xl, 16)
            sp.wait_ge(s_xb, 1)
            sp.dma_start(x_load[:, :, :], x_rows[:, STEPS:2 * STEPS, :]).then_inc(s_xl, 16)
            with sp.Fori(0, NB - 2) as i:
                sp.wait_ge(s_xb, i + 2)
                sp.dma_start(x_load[:, :, :], x_rows[:, bass.ds((i + 2) * STEPS, STEPS), :]).then_inc(s_xl, 16)
                sp.wait_ge(s_or, i + 1)
                sp.dma_start(out_rows[:, bass.ds(i * STEPS, STEPS), :], rows_of(gT, i)).then_inc(s_st, 16)
            for n in range(NB - 2, NB):
                sp.wait_ge(s_or, n + 1)
                sp.dma_start(out_rows[:, n * STEPS:(n + 1) * STEPS, :], rows_of(gT, n)).then_inc(s_st, 16)
            sp.wait_ge(s_st, 16 * NB)

        @block.gpsimd
        def _(pool):
            pool.memset(ident[:, :], 0.0).then_inc(s_ident, 1)
            pool.memset(hu[0:NS, 0, :], 0.0).then_inc(s_h0, 1)
            pool.memset(w_in[:, :, 0:NS], 0.0).then_inc(s_h0, 1)
            pool.memset(ones[:, :], 1.0).then_inc(s_const, 1)
            pool.memset(neg_half[:, :], -0.5).then_inc(s_half, 1)
            pool.wait_ge(s_ident, 1)
            pool.affine_select(out=ident[:, :], in_=ident[:, :], compare_op=ALU.not_equal, fill=1.0, base=0,
                               pattern=[[-1, P]], channel_multiplier=1).then_inc(s_const, 1)
            pool.wait_ge(s_const, 2)
            pool.tensor_copy(ident16[:, :], ident[:, :]).then_inc(s_const, 1)
            pool.dma_start(cd_stage[:, :, 0:NS], C.rearrange("(k p) s -> p k s", p=P)).then_inc(s_wc, 16)
            pool.dma_start(cd_stage[:, :, NS:2 * NS], D.rearrange("(k p) s -> p k s", p=P)).then_inc(s_wc, 16)
            pool.dma_start(w_out[:, :, :], W_out.rearrange("(k p) m -> p k m", p=P)).then_inc(s_wc, 16)
            pool.dma_start(b1_col[:, :], b1.rearrange("(p j) -> p j", j=HC)).then_inc(s_wc, 16)
            pool.dma_start(half_b_out[:, :], b_out.partition_broadcast(P)).then_inc(s_wc, 16)
            pool.dma_start(b2_row[:, :], b2.partition_broadcast(P)).then_inc(s_wc, 16)

            def align(n, first=False):
                for s in range(STEPS):
                    if not (first and s == 0):
                        apart(pool)
                        pool.wait_ge(s_shift, n * STEPS + s)
                    pool.tensor_copy(hu[0:NS, bass.ds(n * STEPS + s, 1), :],
                                     hu[0:NS, bass.ds(n * STEPS + s + 1, 1), :]).then_inc(s_shift, 1)

            def mix(n, first=False):
                for m in range(KD):
                    if m == 0 and not first:
                        apart(pool)
                        pool.wait_ge(s_omm, n * 2)
                    pool.wait_ge(s_t, n * KD + m + 1)
                    pool.tensor_tensor(ysT[:, m, :], gT[:, n, m, :], xT[:, n, m, :], ALU.subtract).then_inc(s_ys, 1)

            def add_bias(n):
                apart(pool)
                pool.wait_ge(s_xl, n * 16 + 16)
                pool.tensor_tensor(x1_rows[:, :, :], x_load[:, :, :],
                                   half_b_out[:, None, :].broadcast_to([P, STEPS, DM]), ALU.add).then_inc(s_xb, 1)

            def residual(n):
                apart(pool)
                pool.wait_ge(s_x1, n * 2 + 2)
                pool.tensor_tensor(rows_of(gT, n), x1_rows[:, :, :],
                                   b2_row[:, None, :].broadcast_to([P, STEPS, DM]), ALU.add).then_inc(s_x1b, 1)

            def second_sum(n):
                apart(pool)
                pool.wait_ge(s_fin, n * STEPS + STEPS)
                pool.wait_ge(s_x1b, n + 1)
                pool.tensor_tensor(rows_of(gT, n), fin[:, :, :], rows_of(gT, n), ALU.add).then_inc(s_r2, 1)

            def first_rstd(n, pair):
                apart(pool)
                pool.wait_ge(s_v1, n * 2 + pair + 1)
                pool.tensor_tensor(rstd[:, 0, 2 * pair:2 * pair + 2], rstd[:, 0, 2 * pair:2 * pair + 2],
                                   neg_half[:, 0:2], ALU.pow).then_inc(s_rs1, 1)

            def second_rstd(n):
                apart(pool)
                pool.wait_ge(s_v2, n + 1)
                pool.tensor_tensor(rstd[:, 1, :], rstd[:, 1, :], neg_half[:, :], ALU.pow).then_inc(s_rs2, 1)

            def iteration(n, stage_a, final, last_a=False):
                if final:
                    second_sum(n - 1)
                if stage_a:
                    mix(n + 1)
                if final:
                    second_rstd(n - 1)
                if stage_a:
                    for pair in range(2):
                        first_rstd(n + 1, pair)
                    if not last_a:
                        align(n + 2)
                    residual(n + 1)
                    if not last_a:
                        pool.wait_ge(s_x1t, n * 2 + 4)
                        pool.wait_ge(s_x1b, n + 2)
                        add_bias(n + 2)

            pool.wait_ge(s_half, 1)
            pool.wait_ge(s_done, 1)
            align(0, first=True)
            pool.wait_ge(s_hb, 1)
            add_bias(0)
            mix(0, first=True)
            for pair in range(2):
                first_rstd(0, pair)
            align(1)
            residual(0)
            pool.wait_ge(s_x1t, 2)
            pool.wait_ge(s_x1b, 1)
            add_bias(1)
            iteration(0, True, False)
            with pool.Fori(1, NB - 2) as i:
                iteration(i, True, True)
            iteration(NB - 2, True, True, last_a=True)
            iteration(NB - 1, False, True)
            second_sum(NB - 1)
            second_rstd(NB - 1)

        @block.scalar
        def _(act):
            act.dma_start(w_in[:, :, NS:P], W_in.rearrange("(k p) s -> p k s", p=P)).then_inc(s_wa, 16)
            act.dma_start(w_rec[0:NS, :], A).then_inc(s_wa, 16)
            act.dma_start(w_rec[NS:P, :], Bm).then_inc(s_wa, 16)
            act.dma_start(b_in_col[NS:P, :], b_in.rearrange("(s a) -> s a", a=1)).then_inc(s_wa, 16)
            act.dma_start(w_gate[:, :, :], W_gate.rearrange("(k p) m -> p k m", p=P)).then_inc(s_wb, 16)
            act.dma_start(b_gate_col[:, :], b_gate.rearrange("(k p) -> p k", p=P),
                          allow_slow_non_contiguous=True).then_inc(s_wb, 16)

            act.wait_ge(s_const, 3)
            nc.scalar.activation(small[0:1, 28:29], ident[0:1, 0:1], ACT.Sigmoid)
            with act.Fori(0, NB) as j:
                for s in range(STEPS):
                    act.wait_ge(s_scan, j * STEPS + s + 1)
                    nc.scalar.activation(hu[0:NS, bass.ds(j * STEPS + s + 1, 1), :],
                                         bank[6 + s % 2][0:NS, None, 0:P], ACT.Tanh).then_inc(s_h, 1)
            def sweep1_block(j):
                for s in range(STEPS):
                    act.wait_ge(s_scan, j * STEPS + L + s + 1)
                    nc.scalar.activation(hu[0:NS, bass.ds(j * STEPS + s + 1, 1), :],
                                         bank[6 + s % 2][0:NS, None, 0:P], ACT.Tanh).then_inc(s_h, 1)
                    if s % 2:
                        m = s // 2
                        act.wait_ge(s_gmm, j * KD + m + 1)
                        nc.scalar.activation(gT[:, j, m, :], bank[m][:, :], ACT.Sigmoid,
                                             bias=b_gate_col[:, m:m + 1]).then_inc(s_g, 1)

            act.wait_ge(s_wb, 32)
            with act.Fori(0, NB - STAGED) as j:
                sweep1_block(j)
            act.wait_ge(s_sgn, 2)
            with act.Fori(NB - STAGED, NB) as j:
                sweep1_block(j)
            for w in range(4):
                act.wait_ge(s_wtp, w + 1)
                src = bank[w][:, :].bitcast(F16)
                if w < 2:
                    nc.scalar.activation(w1s[:, w, :], src, ACT.Copy).then_inc(s_wt, 1)
                else:
                    nc.scalar.activation(w2s[:, (w - 2) * 4:(w - 1) * 4, :].rearrange("p j d -> p (j d)"), src,
                                         ACT.Copy).then_inc(s_wt, 1)
            act.wait_ge(s_wc, 96)
            nc.scalar.mul(half_b_out[:, :], half_b_out[:, :], 0.5).then_inc(s_hb, 1)
            act.wait_ge(s_flag, 1)
            differ = act.value_load(flag_i[0:1, 0:1], min_val=0, max_val=NS)
            with act.If(differ):
                with act.Fori(0, CHUNKS) as r:
                    with act.Fori(0, L // 2) as j:
                        for s in range(2):
                            act.wait_ge(s_rscan, r * L + j * 2 + s + 1)
                            nc.scalar.activation(hu[0:NS, bass.ds(j * 2 + s + 1, 1), :],
                                                 bank[6 + s][0:NS, None, 0:P], ACT.Tanh).then_inc(s_rh, 1)

            def x1_hi(n, pair):
                act.wait_ge(s_x1t, n * 2 + pair + 1)
                nc.scalar.activation(
                    x1T[:, n, 0, 2 * pair:2 * pair + 2].rearrange("p s k r -> p (s k r)"),
                    bank[6 + pair][:, :], ACT.Copy, scale=X_SCALE).then_inc(s_xhi, 1)

            def iteration(n, stage_a, first=False):
                for c in range(HC):
                    b = bank[4 + c % 2]
                    act.wait_ge(s_f1, n * HC + c + 1)
                    nc.scalar.activation(b[:, :], b[:, :], ACT.Gelu, bias=b1_col[:, c:c + 1],
                                         scale=alpha1[:, c:c + 1]).then_inc(s_gelu, 1)
                    act.wait_ge(s_gelu, n * HC + c + 1)
                    if not (first and c < 4):
                        act.wait_ge(s_f2, n * HC + c - 3)
                    nc.scalar.activation(hid[:, c % 4, 0, :], b[:, :], ACT.Copy,
                                         scale=hid_scale[:, 0:1]).then_inc(s_hhi, 1)
                    if stage_a and c >= HC - 2:
                        x1_hi(n + 1, c - (HC - 2))

            act.wait_ge(s_scale, 1)
            x1_hi(0, 0)
            x1_hi(0, 1)
            iteration(0, True, first=True)
            with act.Fori(1, NB - 1) as i:
                iteration(i, True)
            iteration(NB - 1, False)

        @block.tensor
        def _(pe):
            def transpose_step(j, s, slot, wait_bank):
                if wait_bank:
                    pe.wait_ge(s_xtr, j * STEPS - STEPS + s + 1)
                for k in range(KD):
                    done = nc.tensor.transpose(bank[s][:, k * P:(k + 1) * P],
                                               xrow_buf(slot)[:, s, k * P:(k + 1) * P], ident[:, :])
                done.then_inc(s_xt, 1)

            def u_half(j, half, wait_bank):
                pe.wait_ge(s_xtr, j * STEPS + 2 * half + 2)
                if wait_bank:
                    pe.wait_ge(s_u, j * 2 - 2 + half + 1)
                for k in range(KD):
                    done = nc.tensor.matmul(bank[4 + half][:, 0:N // 2], w_in[:, k, :],
                                            xT[:, j, k, half * (N // 2):(half + 1) * (N // 2)],
                                            start=(k == 0), stop=(k == KD - 1))
                done.then_inc(s_umm, 1)

            def scan_step(t, parity, done_sem):
                nc.tensor.matmul(bank[6 + parity][0:NS, 0:P], w_rec[:, :], hu[:, t, :],
                                 start=True, stop=True).then_inc(done_sem, 1)

            pe.wait_ge(s_const, 3)
            pe.wait_ge(s_xin[0], 16)
            for s in range(STEPS):
                transpose_step(0, s, 0, False)
            pe.wait_ge(s_wa, 64)
            pe.wait_ge(s_h0, 2)
            for half in range(2):
                u_half(0, half, False)

            def sweep0_block(j, slot, arrived, first):
                for s in range(STEPS):
                    t = j * STEPS + s
                    pe.wait_ge(s_u, j * 2 + s // 2 + 1)
                    if not (first and s == 0):
                        pe.wait_ge(s_h, t)
                    scan_step(t, s % 2, s_scan)
                    if slot is not None:
                        if s == 0:
                            pe.wait_ge(s_xin[slot], arrived)
                        if s < 2:
                            transpose_step(j + 1, 2 * s, slot, True)
                            transpose_step(j + 1, 2 * s + 1, slot, True)
                        else:
                            u_half(j + 1, s - 2, True)

            for q in range(RING):
                sweep0_block(q, (q + 1) % RING, 16 * ((q + 1) // RING + 1), q == 0)
            with pe.Fori(1, (NB - 1) // RING) as i:
                for q in range(RING):
                    sweep0_block(i * RING + q, (q + 1) % RING, i * 16 + 16 * ((q + 1) // RING + 1), False)
            sweep0_block(NB - 1, None, 0, False)

            pe.wait_ge(s_wb, 32)
            pe.wait_ge(s_guess, 1)

            def sweep1_block(j, first):
                for s in range(STEPS):
                    pe.wait_ge(s_h, j * STEPS + L + s)
                    scan_step(j * STEPS + s, s % 2, s_scan)
                    m, k = divmod(s, 2)
                    if k == 0 and not first:
                        pe.wait_ge(s_g, j * KD - KD + m + 1)
                    done = nc.tensor.matmul(bank[m][:, :], w_gate[:, k, m * P:(m + 1) * P], xT[:, j, k, :],
                                            start=(k == 0), stop=(k == KD - 1))
                    if k == KD - 1:
                        done.then_inc(s_gmm, 1)

            sweep1_block(0, True)
            with pe.Fori(1, NB) as j:
                sweep1_block(j, False)

            pe.wait_ge(s_wc, 96)
            for k in range(KD):
                done = nc.tensor.transpose(bank[4][:, k * P:(k + 1) * P], cd_stage[:, k, :], ident[:, :])
            done.then_inc(s_cdp, 1)
            pe.wait_ge(s_sgn, 2)
            pe.wait_ge(s_g, NB * KD)
            for k in range(KD):
                for j in range(HC):
                    done = nc.tensor.transpose(bank[k][:, :].bitcast(F16)[:, j * P:(j + 1) * P],
                                               w1_sgn[:, j, k * P:(k + 1) * P], ident16[:, :])
                done.then_inc(s_wtp, 1)
            for j in range(HC):
                for k in range(KD):
                    at = (j % 4) * DM + k * P
                    done = nc.tensor.transpose(bank[2 + j // 4][:, :].bitcast(F16)[:, at:at + P],
                                               w2_sgn[:, k, :].rearrange("p (q j) -> p q j", j=HC)[:, :, j],
                                               ident16[:, :])
                if j % 4 == 3:
                    done.then_inc(s_wtp, 1)
            pe.wait_ge(s_dg, 2)
            for k in range(KD):
                done = nc.tensor.matmul(bank[5][:, k * P:(k + 1) * P], ones[:, :], diag[:, k, :], start=True, stop=True)
            done.then_inc(s_a2p, 1)
            pe.wait_ge(s_h, 2 * L)
            pe.wait_ge(s_prep, 4)
            nc.tensor.transpose(bank[7][0:1, 0:P], bound_max, ident[:, :]).then_inc(s_mt, 1)
            pe.wait_ge(s_m1, 1)
            nc.tensor.matmul(bank[7][:, 0:1], ones[0:1, :], bound_all, start=True, stop=True).then_inc(s_mb, 1)

            pe.wait_ge(s_cmp, 3)
            nc.tensor.matmul(bank[6][0:1, 0:1], gap_flag, ones[0:NS, 0:1], start=True, stop=True).then_inc(s_cnt, 1)
            pe.wait_ge(s_flag, 1)
            differ = pe.value_load(flag_i[0:1, 0:1], min_val=0, max_val=NS)
            with pe.If(differ):
                with pe.Fori(0, CHUNKS) as r:
                    with pe.Fori(0, L // 2) as j:
                        for s in range(2):
                            pe.wait_ge(s_rh, r * (L + 1) + j * 2 + s + 1)
                            scan_step(j * 2 + s, s, s_rscan)

            def y_products(n, first=False):
                pe.wait_ge(s_shift, n * STEPS + STEPS)
                if not first:
                    pe.wait_ge(s_xlo, n * 2)
                for m in range(KD):
                    nc.tensor.matmul(bank[6 + m][:, :], cd_t[:, m * P:(m + 1) * P],
                                     hu[:, bass.ds(n * STEPS, STEPS), :].rearrange("p s r -> p (s r)"),
                                     start=True, stop=True).then_inc(s_ymm, 1)

            def out_products(n, pair):
                if pair == 0:
                    pe.wait_ge(s_ys, n * KD + KD)
                for e in range(2):
                    tile = 2 * pair + e
                    for k in range(KD):
                        done = nc.tensor.matmul(bank[6 + pair][:, e * DM:(e + 1) * DM],
                                                ysT[:, k, tile * P:(tile + 1) * P], w_out[:, k, :],
                                                start=(k == 0), stop=(k == KD - 1))
                done.then_inc(s_omm, 1)

            def x1_transposes(n, pair):
                pe.wait_ge(s_x1, n * 2 + pair + 1)
                for e in range(2):
                    for k in range(KD):
                        at = (e * KD + k) * P
                        done = nc.tensor.transpose(bank[6 + pair][:, at:at + P],
                                                   x1_rows[:, 2 * pair + e, k * P:(k + 1) * P], ident[:, :])
                done.then_inc(s_x1t, 1)

            def hidden(n, c, first=False):
                if c == 0:
                    pe.wait_ge(s_xlo, n * 2 + 2)
                if not (first and c < 2):
                    pe.wait_ge(s_hlo, n * HC + c - 1)
                for k in range(KD):
                    for part in range(2):
                        done = nc.tensor.matmul(bank[4 + c % 2][:, :], w1s[:, k, c * P:(c + 1) * P],
                                                x1T[:, n, part, :, k, :],
                                                start=(k == 0 and part == 0), stop=(k == KD - 1 and part == 1))
                done.then_inc(s_f1, 1)

            def ffn_out(n, c, first=False):
                pe.wait_ge(s_hlo, n * HC + c + 1)
                if c == 0 and not first:
                    pe.wait_ge(s_fin, n * STEPS)
                for tile in range(STEPS):
                    for part in range(2):
                        done = nc.tensor.matmul(bank[tile][:, 0:DM], hid[:, c % 4, part, tile * P:(tile + 1) * P],
                                                w2s[:, c, :], start=(c == 0 and part == 0),
                                                stop=(c == HC - 1 and part == 1))
                done.then_inc(s_f2, 1)

            def iteration(n, stage_a, first=False):
                for c in range(HC):
                    if stage_a and c in (3, 4):
                        out_products(n + 1, c - 3)
                    if stage_a and c in (6, 7):
                        x1_transposes(n + 1, c - 6)
                    hidden(n, c, first)
                    if stage_a and c == 0:
                        y_products(n + 1)
                    if c >= 2:
                        ffn_out(n, c - 2, first)
                ffn_out(n, HC - 2)
                ffn_out(n, HC - 1)

            pe.wait_ge(s_cd, 1)
            y_products(0, first=True)
            for pair in range(2):
                out_products(0, pair)
            for pair in range(2):
                x1_transposes(0, pair)
            pe.wait_ge(s_wt, 4)
            pe.wait_ge(s_scale, 1)
            iteration(0, True, first=True)
            with pe.Fori(1, NB - 1) as i:
                iteration(i, True)
            iteration(NB - 1, False)

        @block.vector
        def _(dve):
            def x_out(j, s):
                dve.wait_ge(s_xt, j * STEPS + s + 1)
                nc.vector.tensor_copy(xT[:, j, :, s * P:(s + 1) * P],
                                      bank[s][:, 0:DM].rearrange("p (k r) -> p k r", k=KD)).then_inc(s_xtr, 1)

            def u_out(j, half):
                dve.wait_ge(s_umm, j * 2 + half + 1)
                nc.vector.tensor_scalar(
                    hu[NS:P, bass.ds(j * STEPS + half * 2, 2), :],
                    bank[4 + half][NS:P, 0:N // 2].rearrange("p (s r) -> p s r", r=P),
                    b_in_col[NS:P, :], None, ALU.add).then_inc(s_u, 1)

            dve.wait_ge(s_wa, 64)
            with dve.Fori(0, NB) as j:
                for s in range(STEPS):
                    x_out(j, s)
                for half in range(2):
                    u_out(j, half)
            dve.wait_ge(s_h, L)
            nc.vector.tensor_copy(guess, end_state).then_inc(s_guess, 1)

            dve.wait_ge(s_w12, 32)
            nc.vector.tensor_scalar(neg_w1, w1_stage, 0.0, None, ALU.is_lt)
            nc.vector.tensor_scalar(neg_w2, w2_stage, 0.0, None, ALU.is_lt)
            nc.vector.tensor_reduce(alpha1[:, :], w1_stage, AX.X, ALU.add, apply_absolute_value=True)
            nc.vector.tensor_reduce(alpha2[:, :], w2_stage, AX.X, ALU.add, apply_absolute_value=True).then_inc(s_prep, 1)
            dve.wait_ge(s_prep, 1)
            nc.vector.scalar_tensor_tensor(out=w1_sgn, in0=w1_stage, scalar=0.0, in1=neg_w1, op0=ALU.is_gt,
                                           op1=ALU.subtract).then_inc(s_sgn, 1)
            nc.vector.scalar_tensor_tensor(out=w2_sgn, in0=w2_stage, scalar=0.0, in1=neg_w2, op0=ALU.is_gt,
                                           op1=ALU.subtract).then_inc(s_sgn, 1)
            dve.wait_ge(s_const, 3)
            dve.wait_ge(s_wc, 96)
            for k in range(KD):
                nc.vector.tensor_scalar(diag[:, k, :], ident[:, :], alpha2[:, k:k + 1], 1.0 / H, ALU.mult,
                                        ALU.mult).then_inc(s_dg, 1)
            nc.vector.scalar_tensor_tensor(out=abs_b1, in0=b1_col[:, :], scalar=-1.0, in1=b1_col[:, :], op0=ALU.mult,
                                           op1=ALU.max).then_inc(s_prep, 1)
            dve.wait_ge(s_prep, 2)
            nc.vector.tensor_tensor(bound, alpha1[:, :], abs_b1, ALU.add).then_inc(s_prep, 1)
            dve.wait_ge(s_prep, 3)
            nc.vector.tensor_reduce(bound_max, bound, AX.X, ALU.max).then_inc(s_prep, 1)
            nc.vector.tensor_scalar(alpha1[:, :], alpha1[:, :], 1.0 / (DM * X_SCALE), None, ALU.mult).then_inc(s_prep, 1)

            with dve.Fori(0, NB) as j:
                dve.wait_ge(s_g, j * KD + KD)
                nc.vector.scalar_tensor_tensor(
                    out=xT[:, j].rearrange("p k n -> p (k n)"), in0=gT[:, j].rearrange("p k n -> p (k n)"),
                    scalar=-1.0, in1=xT[:, j].rearrange("p k n -> p (k n)"), op0=ALU.add,
                    op1=ALU.mult).then_inc(s_gx, 1)

            dve.wait_ge(s_h, 2 * L)
            nc.vector.tensor_tensor(gap, end_state, guess, ALU.subtract).then_inc(s_cmp, 1)
            dve.wait_ge(s_cmp, 1)
            nc.vector.tensor_reduce(gap_max, gap, AX.XY, ALU.max, apply_absolute_value=True).then_inc(s_cmp, 1)
            dve.wait_ge(s_cmp, 2)
            nc.vector.tensor_scalar(gap_flag, gap_max, GUESS_TOLERANCE, None, ALU.is_gt).then_inc(s_cmp, 1)
            dve.wait_ge(s_cdp, 1)
            nc.vector.tensor_copy(cd_t[:, :], bank[4][:, 0:DM]).then_inc(s_cd, 1)
            dve.wait_ge(s_mt, 1)
            nc.vector.tensor_reduce(bound_all, bank[7][0:1, 0:P], AX.X, ALU.max).then_inc(s_m1, 1)
            dve.wait_ge(s_mb, 1)
            nc.vector.tensor_scalar(bound_pow, bank[7][:, 0:1], 2.0 ** -100, None, ALU.max).then_inc(s_prep, 1)
            dve.wait_ge(s_prep, 6)
            nc.vector.tensor_single_scalar(bound_pow.bitcast(I32), bound_pow.bitcast(I32), EXPONENT_BITS,
                                           ALU.bitwise_and).then_inc(s_prep, 1)
            dve.wait_ge(s_prep, 7)
            nc.vector.tensor_scalar(inv_scale, bound_pow, 1.0 / TOP, None, ALU.mult).then_inc(s_prep, 1)
            dve.wait_ge(s_prep, 8)
            nc.vector.reciprocal(hid_scale, inv_scale).then_inc(s_prep, 1)
            dve.wait_ge(s_a2p, 1)
            nc.vector.tensor_scalar(alpha2_row[:, :], bank[5][:, 0:DM], inv_scale, None, ALU.mult).then_inc(s_prep, 1)
            dve.wait_ge(s_prep, 10)
            dve.wait_ge(s_cnt, 1)
            nc.vector.tensor_copy(flag_i[:, :], bank[6][0:1, 0:1]).then_inc(s_flag, 1)
            dve.wait_ge(s_flag, 1)
            differ = dve.value_load(flag_i[0:1, 0:1], min_val=0, max_val=NS)
            with dve.If(differ):
                nc.vector.tensor_copy(guess, end_state).then_inc(s_rh, 1)
                with dve.Fori(1, CHUNKS) as r:
                    dve.wait_ge(s_rh, r * (L + 1))
                    nc.vector.tensor_copy(guess, end_state).then_inc(s_rh, 1)
                dve.wait_ge(s_rh, CHUNKS * (L + 1))
            dve.wait_ge(s_gx, NB)
            nc.vector.tensor_copy(small[:, 31:32], inv_scale).then_inc(s_done, 1)
            nc.vector.tensor_copy(small[:, 30:31], inv_scale).then_inc(s_scale, 1)

            def gate_y(n, m):
                dve.wait_ge(s_ymm, n * KD + m + 1)
                nc.vector.tensor_tensor(gT[:, n, m, :], bank[6 + m][:, :], gT[:, n, m, :], ALU.mult).then_inc(s_t, 1)

            def row_stats(which, rows, tiles, at, done_sem):
                for t in tiles:
                    done = nc.vector.bn_stats(stats[:, which, t, :], rows[:, t, :])
                done.then_inc(s_ln, 1)
                dve.wait_ge(s_ln, at + 1)
                nc.vector.memset(small[:, 29:30], 0.0)
                for t in tiles:
                    done = nc.vector.bn_aggr(moments[:, which, t, :], stats[:, which, t, :])
                done.then_inc(s_ln, 1)
                dve.wait_ge(s_ln, at + 2)
                lo, hi = tiles[0], tiles[-1] + 1
                nc.vector.tensor_scalar(rstd[:, which, lo:hi], moments[:, which, lo:hi, 1], LN_EPS, None,
                                        ALU.add).then_inc(done_sem, 1)

            def normalise(which, rows, tiles, done_sem):
                for t in tiles:
                    done = nc.vector.tensor_scalar(rows[:, t, :], rows[:, t, :], moments[:, which, t, 0:1],
                                                   rstd[:, which, t:t + 1], ALU.subtract, ALU.mult)
                done.then_inc(done_sem, 1)

            FIRST = 3
            SECOND = 2
            PER = 2 * FIRST + SECOND

            def first_stats(n, pair, at):
                dve.wait_ge(s_omm, n * 2 + pair + 1)
                dve.wait_ge(s_xb, n + 1)
                for e in range(2):
                    t = 2 * pair + e
                    done = nc.vector.scalar_tensor_tensor(out=x1_rows[:, t, :], in0=x1_rows[:, t, :], scalar=2.0,
                                                          in1=bank[6 + pair][:, e * DM:(e + 1) * DM], op0=ALU.mult,
                                                          op1=ALU.add)
                done.then_inc(s_ln, 1)
                dve.wait_ge(s_ln, at + 1)
                row_stats(0, x1_rows, (2 * pair, 2 * pair + 1), at + 1, s_v1)

            def first_norm(n, pair):
                dve.wait_ge(s_rs1, n * 2 + pair + 1)
                normalise(0, x1_rows, (2 * pair, 2 * pair + 1), s_x1)

            def second_stats(n, at):
                dve.wait_ge(s_r2, n + 1)
                row_stats(1, rows_of(gT, n), range(STEPS), at, s_v2)

            def second_norm(n):
                dve.wait_ge(s_rs2, n + 1)
                normalise(1, rows_of(gT, n), range(STEPS), s_or)

            def x1_lo(n, pair):
                dve.wait_ge(s_xhi, n * 2 + pair + 1)
                nc.vector.scalar_tensor_tensor(
                    out=x1T[:, n, 1, 2 * pair:2 * pair + 2].rearrange("p s k r -> p (s k r)"),
                    in0=bank[6 + pair][:, :], scalar=X_SCALE,
                    in1=x1T[:, n, 0, 2 * pair:2 * pair + 2].rearrange("p s k r -> p (s k r)"),
                    op0=ALU.mult, op1=ALU.subtract).then_inc(s_xlo, 1)

            def hidden_lo(n, c):
                dve.wait_ge(s_hhi, n * HC + c + 1)
                nc.vector.scalar_tensor_tensor(out=hid[:, c % 4, 1, :], in0=bank[4 + c % 2][:, :],
                                               scalar=hid_scale[:, 0:1], in1=hid[:, c % 4, 0, :], op0=ALU.mult,
                                               op1=ALU.subtract).then_inc(s_hlo, 1)

            def ffn_scale(n):
                dve.wait_ge(s_f2, n * HC + HC)
                for t in range(STEPS):
                    nc.vector.tensor_tensor(fin[:, t, :], bank[t][:, 0:DM], alpha2_row[:, :], ALU.mult).then_inc(s_fin, 1)

            def iteration(n, stage_a, final, at):
                if final:
                    ffn_scale(n - 1)
                if stage_a:
                    for m in range(KD):
                        gate_y(n + 1, m)
                for c in range(HC):
                    hidden_lo(n, c)
                    if final and c == 1:
                        second_stats(n - 1, at)
                        at = at + SECOND
                    if stage_a and c in (2, 3):
                        first_stats(n + 1, c - 2, at)
                        at = at + FIRST
                    if final and c == 3:
                        second_norm(n - 1)
                    if stage_a and c in (4, 5):
                        first_norm(n + 1, c - 4)
                    if stage_a and c >= HC - 2:
                        x1_lo(n + 1, c - (HC - 2))

            for m in range(KD):
                gate_y(0, m)
            first_stats(0, 0, 0)
            first_stats(0, 1, FIRST)
            first_norm(0, 0)
            first_norm(0, 1)
            x1_lo(0, 0)
            x1_lo(0, 1)
            iteration(0, True, False, 2 * FIRST)
            with dve.Fori(1, NB - 1) as i:
                iteration(i, True, True, i * PER + (4 * FIRST - PER))
            at = 4 * FIRST + (NB - 2) * PER
            iteration(NB - 1, False, True, at)
            ffn_scale(NB - 1)
            second_stats(NB - 1, at + SECOND)
            second_norm(NB - 1)


_INS = ['L0_attn_x', 'L0_attn_W_in', 'L0_attn_b_in', 'L0_attn_W_gate', 'L0_attn_b_gate', 'L0_attn_A', 'L0_attn_Bm',
        'L0_attn_C', 'L0_attn_D', 'L0_attn_W_out', 'L0_attn_b_out', 'L0_ffn_w1', 'L0_ffn_b1', 'L0_ffn_w2', 'L0_ffn_b2']


def kernel(**inputs):
    import numpy as _np
    import concourse.bacc as _bacc
    from concourse import mybir as _mybir
    from concourse.bass_utils import run_bass_kernel_spmd as _run

    nc = _bacc.Bacc("TRN2", target_bir_lowering=False, num_devices=1)
    arrays, args = {}, []
    for name in _INS:
        a = _np.ascontiguousarray(inputs[name])
        arrays[f"in_{name}"] = a
        args.append(nc.dram_tensor(f"in_{name}", a.shape, _mybir.dt.from_np(a.dtype), kind="ExternalInput").ap())
    shape = arrays["in_L0_attn_x"].shape
    args.append(nc.dram_tensor("out_rows", shape, _mybir.dt.float32, kind="ExternalOutput").ap())
    gated_rnn_ffn(nc, *args)
    r = _run(nc, [arrays], core_ids=[0])
    return r.results[0]["out_rows"]
```

```python
from contextlib import ExitStack

import concourse.bass as bass
from concourse import mybir

F32 = mybir.dt.float32
F16 = mybir.dt.float16
I32 = mybir.dt.int32
ALU = mybir.AluOpType
ACT = mybir.ActivationFunctionType
AX = mybir.AxisListType

P = 128
STEPS = 4
RING = 5
WARM = 44
LN_EPS = 1e-5
GUESS_TOLERANCE = 2.0 ** -18
X_SCALE = 1024.0
TOP = 2.0 ** 14
EXPONENT_BITS = 0x7F800000


def gated_rnn_ffn(nc, x, W_in, b_in, W_gate, b_gate, A, Bm, C, D, W_out, b_out, w1, b1, w2, b2, out):
    BATCH, T, DM = x.shape
    NS = A.shape[0]
    H = w1.shape[0]
    KD = DM // P
    HC = H // P
    CHUNKS = P // BATCH
    L = T // CHUNKS
    NB = L // STEPS
    N = STEPS * P
    T0 = L - WARM
    B0 = T0 // STEPS
    LATE = 4
    GATED = NB - LATE
    assert NS == 64 and KD == 2 and L % STEPS == 0 and T0 % STEPS == 0 and N == 512 and HC == 8
    assert B0 == RING and (NB - 1 - B0) % RING == 0

    x_rows = x.rearrange("b (c s) d -> (b c) s d", s=L)
    out_rows = out.rearrange("b (c s) d -> (b c) s d", s=L)

    with ExitStack() as ctx:
        def sb(name, shape, dt=F32):
            return ctx.enter_context(nc.sbuf_tensor(name, shape, dt))

        def sem(name):
            return ctx.enter_context(nc.semaphore(name))

        xT = sb("xT", [P, NB, KD, N])
        gT = sb("gT", [P, NB, KD, N])
        hu = sb("hu", [P, L + 1, P])
        w_in = sb("w_in", [P, KD, P])
        w_gate = sb("w_gate", [P, KD, DM])
        w_out = sb("w_out", [P, KD, DM])
        w_rec = sb("w_rec", [P, NS])
        cd_t = sb("cd_t", [P, DM])
        w1s = sb("w1s", [P, KD, H], F16)
        w2s = sb("w2s", [P, HC, DM], F16)
        b_in_col = sb("b_in_col", [P, 1])
        b_gate_col = sb("b_gate_col", [P, KD])
        b1_col = sb("b1_col", [P, HC])
        alpha1 = sb("alpha1", [P, HC])
        alpha2 = sb("alpha2", [P, KD])
        alpha2_row = sb("alpha2_row", [P, DM])
        half_b_out = sb("half_b_out", [P, DM])
        b2_row = sb("b2_row", [P, DM])
        ident = sb("ident", [P, P])
        ident16 = sb("ident16", [P, P], F16)
        small = sb("small", [P, 32])
        neg_half = sb("neg_half", [P, STEPS])
        flag_i = sb("flag_i", [1, 1], I32)
        ysT = sb("ysT", [P, KD, N])
        x_load = sb("x_load", [P, STEPS, DM])
        x1_rows = sb("x1_rows", [P, STEPS, DM])
        g32 = sb("g32", [P, 2, N])
        hid = sb("hid", [P, 4, 2, N], F16)
        fin = sb("fin", [P, STEPS, DM])
        stats = sb("stats", [P, 2, STEPS, 6])
        moments = sb("moments", [P, 2, STEPS, 2])
        rstd = sb("rstd", [P, 2, STEPS])

        bank = [ctx.enter_context(nc.psum_tensor(f"bank{i}", [P, N], F32)) for i in range(8)]

        s_wa = sem("first_weights_in")
        s_wb = sem("gate_weights_in")
        s_wc = sem("late_weights_in")
        s_w12 = sem("ffn_weights_in")
        s_x0 = [sem(f"first_step_in{i}") for i in range(STEPS)]
        s_xin = [sem(f"x_block_in{i}") for i in range(RING)]
        s_const = sem("constants_ready")
        s_ident = sem("identity_steps")
        s_half = sem("exponent_ready")
        s_h0 = sem("initial_state_ready")
        s_xt = sem("x_transposed")
        s_xtr = sem("xT_ready")
        s_umm = sem("u_product")
        s_u = sem("u_ready")
        s_scan = sem("scan_product")
        s_h = sem("state_ready")
        s_guess = sem("guess_set")
        s_gmm = sem("gate_product")
        s_g = sem("gate_ready")
        s_gx = sem("gated_x_ready")
        s_cmp = sem("compare_steps")
        s_cnt = sem("mismatches_counted")
        s_flag = sem("flag_ready")
        s_rscan = sem("repair_product")
        s_rh = sem("repair_state")
        s_done = sem("states_final")
        s_prep = sem("prep_chain")
        s_sgn = sem("signs_ready")
        s_cdp = sem("cd_transposed")
        s_cd = sem("cd_ready")
        s_wtp = sem("signs_transposed")
        s_wt = sem("sign_weights_ready")
        s_mt = sem("bound_transposed")
        s_m1 = sem("bound_reduced")
        s_mb = sem("bound_broadcast")
        s_a2p = sem("alpha2_broadcast")
        s_a2 = sem("alpha2_row_ready")
        s_dg = sem("alpha2_diagonal")
        s_scale = sem("scales_ready")
        s_hb = sem("half_bias_ready")
        s_shift = sem("states_aligned")
        s_ymm = sem("y_product")
        s_t = sem("gated_y_ready")
        s_ys = sem("ys_ready")
        s_omm = sem("out_product")
        s_xl = sem("x_reloaded")
        s_xb = sem("x_plus_bias_ready")
        s_ln = sem("norm_chain")
        s_v1 = sem("first_variance_ready")
        s_rs1 = sem("first_rstd_ready")
        s_v2 = sem("second_variance_ready")
        s_rs2 = sem("second_rstd_ready")
        s_x1 = sem("x1_ready")
        s_x1t = sem("x1_transposed")
        s_xhi = sem("x1_hi_ready")
        s_xlo = sem("x1_lo_ready")
        s_x1b = sem("residual_ready")
        s_f1 = sem("hidden_product")
        s_gelu = sem("gelu_ready")
        s_hhi = sem("hidden_hi_ready")
        s_hlo = sem("hidden_lo_ready")
        s_f2 = sem("ffn_product")
        s_fin = sem("ffn_sum_ready")
        s_r2 = sem("ffn_residual_ready")
        s_or = sem("out_ready")
        s_st = sem("out_stored")

        def xrow_buf(slot):
            return gT[:, slot].rearrange("p k n -> p (k n)").rearrange("p (s d) -> p s d", d=DM)

        def rows_of(buf, n):
            return buf[:, n].rearrange("p k n -> p (k n)").rearrange("p (s d) -> p s d", d=DM)

        x1T = xT[:, :, :, :].rearrange("p b k n -> p b (k n)").bitcast(F16).rearrange(
            "p b (h s k r) -> p b h s k r", h=2, s=STEPS, k=KD)
        STAGED = 4
        w1_stage = gT[:, NB - 2:NB].rearrange("p b k n -> p (b k n)").rearrange("p (j d) -> p j d", d=DM)
        w2_stage = gT[:, NB - STAGED:NB - 2].rearrange("p b k n -> p (b k n)").rearrange("p (k h) -> p k h", k=KD)
        w1_sgn = hid[:, 0:2].rearrange("p a b n -> p (a b n)").rearrange("p (j d) -> p j d", d=DM)
        w2_sgn = hid[:, 2:4].rearrange("p a b n -> p (a b n)").rearrange("p (k h) -> p k h", k=KD)
        neg_w1 = ysT[:, :, :].rearrange("p k n -> p (k n)").bitcast(F16).rearrange("p (j d) -> p j d", d=DM)
        neg_w2 = fin[:, :, :].rearrange("p a b -> p (a b)").bitcast(F16).rearrange("p (k h) -> p k h", k=KD)
        cd_stage = x1_rows[:, 0:1, :].rearrange("p a (k n) -> p (a k) n", k=KD)
        diag = x1_rows[:, 1:2, :].rearrange("p a (k n) -> p (a k) n", k=KD)
        end_state = hu[0:NS, L, :].rearrange("p (b c) -> p b c", b=BATCH)[:, :, 0:CHUNKS - 1]
        guess = hu[0:NS, 0, :].rearrange("p (b c) -> p b c", b=BATCH)[:, :, 1:CHUNKS]
        gap = x_load[0:NS, 0, 0:P - BATCH].rearrange("p (b c) -> p b c", b=BATCH)
        ones = x_load[:, 1, 0:P]
        gap_max = small[0:NS, 0:1]
        gap_flag = small[0:NS, 1:2]
        bound = small[:, 2:2 + HC]
        bound_max = small[:, 10:11]
        bound_all = small[0:1, 11:12]
        inv_scale = small[:, 12:13]
        hid_scale = small[:, 13:14]
        bound_pow = small[:, 14:15]
        abs_b1 = small[:, 16:16 + HC]

        def apart(eng):
            eng.wait_ge(s_const, 3)

        block = ctx.enter_context(nc.Block())

        @block.sync
        def _(sp):
            for s in range(STEPS):
                sp.dma_start(xrow_buf(0)[:, s, :], x_rows[:, s, :]).then_inc(s_x0[s], 16)
            for j in range(1, RING):
                sp.dma_start(xrow_buf(j), x_rows[:, j * STEPS:(j + 1) * STEPS, :]).then_inc(s_xin[j], 16)
            with sp.Fori(0, (NB - 1) // RING - 1) as i:
                for q in range(RING):
                    sp.wait_ge(s_xt, i * (RING * STEPS) + (q + 1) * STEPS)
                    sp.dma_start(xrow_buf(q), x_rows[:, bass.ds(i * (RING * STEPS) + (RING + q) * STEPS, STEPS), :]
                                 ).then_inc(s_xin[q], 16)
            sp.wait_ge(s_xt, (NB - RING) * STEPS)
            sp.dma_start(xrow_buf(0), x_rows[:, L - STEPS:L, :]).then_inc(s_xin[0], 16)
            sp.wait_ge(s_xt, L - 2 * STEPS)
            sp.dma_start(w1_stage, w1.rearrange("(p j) d -> p j d", j=HC)).then_inc(s_w12, 16)
            sp.dma_start(w2_stage, w2.rearrange("(k p) h -> p k h", p=P)).then_inc(s_w12, 16)
            sp.wait_ge(s_done, 1)
            sp.dma_start(x_load[:, :, :], x_rows[:, 0:STEPS, :]).then_inc(s_xl, 16)
            for n in range(1, 4):
                sp.wait_ge(s_xb, n)
                sp.dma_start(x_load[:, :, :], x_rows[:, n * STEPS:(n + 1) * STEPS, :]).then_inc(s_xl, 16)
            with sp.Fori(0, NB - 4) as i:
                sp.wait_ge(s_or, i + 1)
                sp.dma_start(out_rows[:, bass.ds(i * STEPS, STEPS), :], rows_of(gT, i)).then_inc(s_st, 16)
                sp.wait_ge(s_xb, i + 4)
                sp.dma_start(x_load[:, :, :], x_rows[:, bass.ds((i + 4) * STEPS, STEPS), :]).then_inc(s_xl, 16)
            for n in range(NB - 4, NB - 1):
                sp.wait_ge(s_or, n + 1)
                sp.dma_start(out_rows[:, n * STEPS:(n + 1) * STEPS, :], rows_of(gT, n)).then_inc(s_st, 16)
            for pair in range(2):
                sp.wait_ge(s_or, NB + pair)
                at = L - STEPS + 2 * pair
                sp.dma_start(out_rows[:, at:at + 2, :], rows_of(gT, NB - 1)[:, 2 * pair:2 * pair + 2, :]).then_inc(s_st, 16)
            sp.wait_ge(s_st, 16 * (NB + 1))

        @block.gpsimd
        def _(pool):
            pool.memset(ident[:, :], 0.0).then_inc(s_ident, 1)
            pool.memset(hu[0:NS, 0, :], 0.0).then_inc(s_h0, 1)
            pool.memset(hu[0:NS, T0, :], 0.0).then_inc(s_h0, 1)
            pool.memset(w_in[:, :, 0:NS], 0.0).then_inc(s_h0, 1)
            pool.memset(ones, 1.0).then_inc(s_const, 1)
            pool.memset(neg_half[:, :], -0.5).then_inc(s_half, 1)
            pool.wait_ge(s_ident, 1)
            pool.affine_select(out=ident[:, :], in_=ident[:, :], compare_op=ALU.not_equal, fill=1.0, base=0,
                               pattern=[[-1, P]], channel_multiplier=1).then_inc(s_const, 1)
            pool.wait_ge(s_const, 2)
            pool.tensor_copy(ident16[:, :], ident[:, :]).then_inc(s_const, 1)
            pool.dma_start(cd_stage[:, :, 0:NS], C.rearrange("(k p) s -> p k s", p=P)).then_inc(s_wc, 16)
            pool.dma_start(cd_stage[:, :, NS:2 * NS], D.rearrange("(k p) s -> p k s", p=P)).then_inc(s_wc, 16)
            pool.dma_start(w_out[:, :, :], W_out.rearrange("(k p) m -> p k m", p=P)).then_inc(s_wc, 16)
            pool.dma_start(b1_col[:, :], b1.rearrange("(p j) -> p j", j=HC)).then_inc(s_wc, 16)
            pool.dma_start(half_b_out[:, :], b_out.partition_broadcast(P)).then_inc(s_wc, 16)
            pool.dma_start(b2_row[:, :], b2.partition_broadcast(P)).then_inc(s_wc, 16)

            def align(n, first=False):
                for s in range(STEPS):
                    if not (first and s == 0):
                        apart(pool)
                        pool.wait_ge(s_shift, n * STEPS + s)
                    pool.tensor_copy(hu[0:NS, bass.ds(n * STEPS + s, 1), :],
                                     hu[0:NS, bass.ds(n * STEPS + s + 1, 1), :]).then_inc(s_shift, 1)

            def mix(n, first=False):
                for m in range(KD):
                    if m == 0 and not first:
                        apart(pool)
                        pool.wait_ge(s_omm, n * 2)
                    pool.wait_ge(s_t, n * KD + m + 1)
                    pool.tensor_tensor(ysT[:, m, :], gT[:, n, m, :], xT[:, n, m, :], ALU.subtract).then_inc(s_ys, 1)

            def add_bias(n):
                apart(pool)
                pool.wait_ge(s_xl, n * 16 + 16)
                pool.tensor_tensor(x1_rows[:, :, :], x_load[:, :, :],
                                   half_b_out[:, None, :].broadcast_to([P, STEPS, DM]), ALU.add).then_inc(s_xb, 1)

            def residual(n):
                apart(pool)
                pool.wait_ge(s_x1, n * 2 + 2)
                pool.tensor_tensor(rows_of(gT, n), x1_rows[:, :, :],
                                   b2_row[:, None, :].broadcast_to([P, STEPS, DM]), ALU.add).then_inc(s_x1b, 1)

            def second_sum(n):
                apart(pool)
                pool.wait_ge(s_fin, n * STEPS + STEPS)
                pool.wait_ge(s_x1b, n + 1)
                pool.tensor_tensor(rows_of(gT, n), fin[:, :, :], rows_of(gT, n), ALU.add).then_inc(s_r2, 1)

            def first_rstd(n, pair):
                apart(pool)
                pool.wait_ge(s_v1, n * 2 + pair + 1)
                pool.tensor_tensor(rstd[:, 0, 2 * pair:2 * pair + 2], rstd[:, 0, 2 * pair:2 * pair + 2],
                                   neg_half[:, 0:2], ALU.pow).then_inc(s_rs1, 1)

            def second_rstd(n):
                apart(pool)
                pool.wait_ge(s_v2, n + 1)
                pool.tensor_tensor(rstd[:, 1, :], rstd[:, 1, :], neg_half[:, :], ALU.pow).then_inc(s_rs2, 1)

            def iteration(n, stage_a, final, last_a=False):
                if stage_a:
                    mix(n + 1)
                if final:
                    second_sum(n - 1)
                if stage_a:
                    if not last_a:
                        align(n + 2)
                    for pair in range(2):
                        first_rstd(n + 1, pair)
                if final:
                    second_rstd(n - 1)
                if stage_a:
                    residual(n + 1)
                    if not last_a:
                        pool.wait_ge(s_x1t, n * 2 + 4)
                        pool.wait_ge(s_x1b, n + 2)
                        add_bias(n + 2)

            pool.wait_ge(s_half, 1)
            pool.wait_ge(s_done, 1)
            align(0, first=True)
            pool.wait_ge(s_hb, 1)
            add_bias(0)
            mix(0, first=True)
            for pair in range(2):
                first_rstd(0, pair)
            align(1)
            residual(0)
            pool.wait_ge(s_x1t, 2)
            pool.wait_ge(s_x1b, 1)
            add_bias(1)
            iteration(0, True, False)
            with pool.Fori(1, NB - 2) as i:
                iteration(i, True, True)
            iteration(NB - 2, True, True, last_a=True)
            iteration(NB - 1, False, True)
            for pair in range(2):
                tiles = slice(2 * pair, 2 * pair + 2)
                pool.wait_ge(s_v2, NB + pair)
                pool.tensor_tensor(rstd[:, 1, tiles], rstd[:, 1, tiles], neg_half[:, 0:2], ALU.pow).then_inc(s_rs2, 1)

        @block.scalar
        def _(act):
            act.dma_start(w_in[:, :, NS:P], W_in.rearrange("(k p) s -> p k s", p=P)).then_inc(s_wa, 16)
            act.dma_start(w_rec[0:NS, :], A).then_inc(s_wa, 16)
            act.dma_start(w_rec[NS:P, :], Bm).then_inc(s_wa, 16)
            act.dma_start(b_in_col[NS:P, :], b_in.rearrange("(s a) -> s a", a=1)).then_inc(s_wa, 16)
            act.dma_start(w_gate[:, :, :], W_gate.rearrange("(k p) m -> p k m", p=P)).then_inc(s_wb, 16)
            act.dma_start(b_gate_col[:, :], b_gate.rearrange("(k p) -> p k", p=P),
                          allow_slow_non_contiguous=True).then_inc(s_wb, 16)

            act.wait_ge(s_const, 3)
            nc.scalar.activation(small[0:1, 28:29], ident[0:1, 0:1], ACT.Sigmoid)
            with act.Fori(B0, NB) as j:
                for s in range(STEPS):
                    act.wait_ge(s_scan, j * STEPS + (s + 1 - T0))
                    nc.scalar.activation(hu[0:NS, bass.ds(j * STEPS + s + 1, 1), :],
                                         bank[6 + s % 2][0:NS, None, 0:P], ACT.Tanh).then_inc(s_h, 1)

            def gate(j, m):
                act.wait_ge(s_gmm, j * KD + m + 1)
                nc.scalar.activation(gT[:, j, m, :], bank[m][:, :], ACT.Sigmoid,
                                     bias=b_gate_col[:, m:m + 1]).then_inc(s_g, 1)

            def sweep1_block(j, before, own):
                for s in range(STEPS):
                    act.wait_ge(s_scan, j * STEPS + (WARM + s + 1))
                    nc.scalar.activation(hu[0:NS, bass.ds(j * STEPS + s + 1, 1), :],
                                         bank[6 + s % 2][0:NS, None, 0:P], ACT.Tanh).then_inc(s_h, 1)
                    if s == 0 and before:
                        gate(j - 1, 1)
                    if s == 2 and own:
                        gate(j, 0)

            act.wait_ge(s_wb, 32)
            sweep1_block(0, False, True)
            with act.Fori(1, GATED) as j:
                sweep1_block(j, True, True)
            sweep1_block(GATED, True, False)
            with act.Fori(GATED + 1, NB) as j:
                sweep1_block(j, False, False)
            act.wait_ge(s_sgn, 2)
            for w in range(4):
                act.wait_ge(s_wtp, w + 1)
                src = bank[2 + w][:, :].bitcast(F16)
                if w < 2:
                    nc.scalar.activation(w1s[:, w, :], src, ACT.Copy).then_inc(s_wt, 1)
                else:
                    nc.scalar.activation(w2s[:, (w - 2) * 4:(w - 1) * 4, :].rearrange("p j d -> p (j d)"), src,
                                         ACT.Copy).then_inc(s_wt, 1)
            act.wait_ge(s_wc, 96)
            nc.scalar.mul(half_b_out[:, :], half_b_out[:, :], 0.5).then_inc(s_hb, 1)
            for m in range(KD):
                gate(GATED, m)
            act.wait_ge(s_flag, 1)
            differ = act.value_load(flag_i[0:1, 0:1], min_val=0, max_val=NS)
            with act.If(differ):
                with act.Fori(0, CHUNKS) as r:
                    with act.Fori(0, L // 2) as j:
                        for s in range(2):
                            act.wait_ge(s_rscan, r * L + j * 2 + s + 1)
                            nc.scalar.activation(hu[0:NS, bass.ds(j * 2 + s + 1, 1), :],
                                                 bank[6 + s][0:NS, None, 0:P], ACT.Tanh).then_inc(s_rh, 1)

            def x1_hi(n, pair):
                act.wait_ge(s_x1t, n * 2 + pair + 1)
                nc.scalar.activation(
                    x1T[:, n, 0, 2 * pair:2 * pair + 2].rearrange("p s k r -> p (s k r)"),
                    bank[6 + pair][:, :], ACT.Copy, scale=X_SCALE).then_inc(s_xhi, 1)

            def iteration(n, stage_a, first=False):
                for c in range(HC):
                    act.wait_ge(s_f1, n * HC + c + 1)
                    if not (first and c < 2):
                        act.wait_ge(s_hlo, n * HC + c - 1)
                    nc.scalar.activation(g32[:, c % 2, :], bank[4 + c % 2][:, :], ACT.Gelu, bias=b1_col[:, c:c + 1],
                                         scale=alpha1[:, c:c + 1]).then_inc(s_gelu, 1)
                    act.wait_ge(s_gelu, n * HC + c + 1)
                    if not (first and c < 4):
                        act.wait_ge(s_f2, n * HC + c - 3)
                    nc.scalar.activation(hid[:, c % 4, 0, :], g32[:, c % 2, :], ACT.Copy,
                                         scale=hid_scale[:, 0:1]).then_inc(s_hhi, 1)
                    if stage_a and c in (5, 6):
                        x1_hi(n + 1, c - 5)

            for n in range(GATED + 1, NB):
                for m in range(KD):
                    gate(n, m)
            act.wait_ge(s_scale, 1)
            x1_hi(0, 0)
            x1_hi(0, 1)
            iteration(0, True, first=True)
            with act.Fori(1, NB - 1) as i:
                iteration(i, True)
            iteration(NB - 1, False)

        @block.tensor
        def _(pe):
            def transpose_step(j, s, slot, wait_bank):
                if wait_bank:
                    pe.wait_ge(s_xtr, j * STEPS - STEPS + s + 1)
                for k in range(KD):
                    done = nc.tensor.transpose(bank[s][:, k * P:(k + 1) * P],
                                               xrow_buf(slot)[:, s, k * P:(k + 1) * P], ident[:, :])
                done.then_inc(s_xt, 1)

            def u_part(j, half, k, wait_bank):
                if k == 0:
                    pe.wait_ge(s_xtr, j * STEPS + 2 * half + 2)
                    if wait_bank:
                        pe.wait_ge(s_u, j * 2 - 2 + half + 1)
                done = nc.tensor.matmul(bank[4 + half][:, 0:N // 2], w_in[:, k, :],
                                        xT[:, j, k, half * (N // 2):(half + 1) * (N // 2)],
                                        start=(k == 0), stop=(k == KD - 1))
                if k == KD - 1:
                    done.then_inc(s_umm, 1)

            def scan_step(t, parity, done_sem):
                nc.tensor.matmul(bank[6 + parity][0:NS, 0:P], w_rec[:, :], hu[:, t, :],
                                 start=True, stop=True).then_inc(done_sem, 1)

            def arrived(j):
                return 16 * (j // RING + (1 if j % RING else 0))

            pe.wait_ge(s_const, 2)
            for j in range(B0 + 1):
                if j > 0:
                    pe.wait_ge(s_xin[j % RING], arrived(j))
                for s in range(STEPS):
                    if j == 0:
                        pe.wait_ge(s_x0[s], 16)
                    transpose_step(j, s, j % RING, j > 0)
                if j == 0:
                    pe.wait_ge(s_wa, 64)
                    pe.wait_ge(s_h0, 3)
                for half in range(2):
                    for k in range(KD):
                        u_part(j, half, k, j > 0)

            def sweep0_block(j, slot, loads, first):
                for s in range(STEPS):
                    pe.wait_ge(s_u, j * 2 + s // 2 + 1)
                    if not (first and s == 0):
                        pe.wait_ge(s_h, j * STEPS + (s - T0))
                    scan_step(j * STEPS + s, s % 2, s_scan)
                    if slot is None:
                        continue
                    if s == 0:
                        pe.wait_ge(s_xin[slot], loads)
                        for tile in range(3):
                            transpose_step(j + 1, tile, slot, True)
                    if s == 1:
                        transpose_step(j + 1, 3, slot, True)
                        u_part(j + 1, 0, 0, True)
                    if s == 2:
                        u_part(j + 1, 0, 1, True)
                        u_part(j + 1, 1, 0, True)
                    if s == 3:
                        u_part(j + 1, 1, 1, True)

            for q in range(RING):
                sweep0_block(B0 + q, (B0 + q + 1) % RING, arrived(B0 + q + 1), q == 0)
            with pe.Fori(1, (NB - 1 - B0) // RING) as i:
                for q in range(RING):
                    sweep0_block(i * RING + (B0 + q), (B0 + q + 1) % RING, i * 16 + arrived(B0 + q + 1), False)
            sweep0_block(NB - 1, None, 0, False)

            def gate_product(j, m, k, first=False):
                if k == 0 and not first:
                    pe.wait_ge(s_g, j * KD - KD + m + 1)
                done = nc.tensor.matmul(bank[m][:, :], w_gate[:, k, m * P:(m + 1) * P], xT[:, j, k, :],
                                        start=(k == 0), stop=(k == KD - 1))
                if k == KD - 1:
                    done.then_inc(s_gmm, 1)

            def gate_block(j):
                for m in range(KD):
                    for k in range(KD):
                        gate_product(j, m, k)

            pe.wait_ge(s_wb, 32)
            pe.wait_ge(s_guess, 1)

            def sweep1_block(j, gated, first=False):
                for s in range(STEPS):
                    pe.wait_ge(s_h, j * STEPS + (WARM + s))
                    scan_step(j * STEPS + s, s % 2, s_scan)
                    if gated:
                        gate_product(j, s // 2, s % 2, first)

            sweep1_block(0, True, first=True)
            with pe.Fori(1, GATED) as j:
                sweep1_block(j, True)
            with pe.Fori(GATED, NB) as j:
                sweep1_block(j, False)

            pe.wait_ge(s_wc, 96)
            pe.wait_ge(s_g, GATED * KD)
            for k in range(KD):
                done = nc.tensor.transpose(bank[1][:, k * P:(k + 1) * P], cd_stage[:, k, :], ident[:, :])
            done.then_inc(s_cdp, 1)
            pe.wait_ge(s_sgn, 2)
            pe.wait_ge(s_h, WARM + L)
            for k in range(KD):
                for j in range(HC):
                    done = nc.tensor.transpose(bank[2 + k][:, :].bitcast(F16)[:, j * P:(j + 1) * P],
                                               w1_sgn[:, j, k * P:(k + 1) * P], ident16[:, :])
                done.then_inc(s_wtp, 1)
            for j in range(HC):
                for k in range(KD):
                    at = (j % 4) * DM + k * P
                    done = nc.tensor.transpose(bank[4 + j // 4][:, :].bitcast(F16)[:, at:at + P],
                                               w2_sgn[:, k, :].rearrange("p (q j) -> p q j", j=HC)[:, :, j],
                                               ident16[:, :])
                if j % 4 == 3:
                    done.then_inc(s_wtp, 1)
            pe.wait_ge(s_dg, 2)
            for k in range(KD):
                done = nc.tensor.matmul(bank[0][:, k * P:(k + 1) * P], ones, diag[:, k, :], start=True, stop=True)
            done.then_inc(s_a2p, 1)
            pe.wait_ge(s_prep, 4)
            nc.tensor.transpose(bank[7][0:1, 0:P], bound_max, ident[:, :]).then_inc(s_mt, 1)
            pe.wait_ge(s_m1, 1)
            nc.tensor.matmul(bank[7][:, 0:1], x_load[0:1, 1, 0:P], bound_all, start=True, stop=True).then_inc(s_mb, 1)

            pe.wait_ge(s_cmp, 3)
            nc.tensor.matmul(bank[6][0:1, 0:1], gap_flag, x_load[0:NS, 1, 0:1], start=True, stop=True).then_inc(s_cnt, 1)
            pe.wait_ge(s_cd, 1)
            pe.wait_ge(s_a2, 1)
            gate_block(GATED)
            pe.wait_ge(s_flag, 1)
            differ = pe.value_load(flag_i[0:1, 0:1], min_val=0, max_val=NS)
            with pe.If(differ):
                with pe.Fori(0, CHUNKS) as r:
                    with pe.Fori(0, L // 2) as j:
                        for s in range(2):
                            pe.wait_ge(s_rh, r * (L + 1) + j * 2 + s + 1)
                            scan_step(j * 2 + s, s, s_rscan)

            def y_products(n, first=False):
                pe.wait_ge(s_shift, n * STEPS + STEPS)
                if not first:
                    pe.wait_ge(s_xlo, n * 2)
                for m in range(KD):
                    nc.tensor.matmul(bank[6 + m][:, :], cd_t[:, m * P:(m + 1) * P],
                                     hu[:, bass.ds(n * STEPS, STEPS), :].rearrange("p s r -> p (s r)"),
                                     start=True, stop=True).then_inc(s_ymm, 1)

            def out_products(n, pair):
                if pair == 0:
                    pe.wait_ge(s_ys, n * KD + KD)
                for e in range(2):
                    tile = 2 * pair + e
                    for k in range(KD):
                        done = nc.tensor.matmul(bank[6 + pair][:, e * DM:(e + 1) * DM],
                                                ysT[:, k, tile * P:(tile + 1) * P], w_out[:, k, :],
                                                start=(k == 0), stop=(k == KD - 1))
                done.then_inc(s_omm, 1)

            def x1_transposes(n, pair):
                pe.wait_ge(s_x1, n * 2 + pair + 1)
                for e in range(2):
                    for k in range(KD):
                        at = (e * KD + k) * P
                        done = nc.tensor.transpose(bank[6 + pair][:, at:at + P],
                                                   x1_rows[:, 2 * pair + e, k * P:(k + 1) * P], ident[:, :])
                done.then_inc(s_x1t, 1)

            def hidden(n, c, first=False):
                if c == 0:
                    pe.wait_ge(s_xlo, n * 2 + 2)
                if not (first and c < 2):
                    pe.wait_ge(s_gelu, n * HC + c - 1)
                for k in range(KD):
                    for part in range(2):
                        done = nc.tensor.matmul(bank[4 + c % 2][:, :], w1s[:, k, c * P:(c + 1) * P],
                                                x1T[:, n, part, :, k, :],
                                                start=(k == 0 and part == 0), stop=(k == KD - 1 and part == 1))
                done.then_inc(s_f1, 1)

            def ffn_out(n, c, first=False):
                pe.wait_ge(s_hlo, n * HC + c + 1)
                if c == 0 and not first:
                    pe.wait_ge(s_fin, n * STEPS)
                for tile in range(STEPS):
                    for part in range(2):
                        done = nc.tensor.matmul(bank[tile][:, 0:DM], hid[:, c % 4, part, tile * P:(tile + 1) * P],
                                                w2s[:, c, :], start=(c == 0 and part == 0),
                                                stop=(c == HC - 1 and part == 1))
                done.then_inc(s_f2, 1)

            def iteration(n, stage_a, first=False):
                for c in range(HC):
                    hidden(n, c, first)
                    if c == 0:
                        if stage_a:
                            y_products(n + 1)
                        if not first:
                            ffn_out(n - 1, HC - 1)
                    if stage_a and c in (2, 3):
                        out_products(n + 1, c - 2)
                    if c >= 2:
                        ffn_out(n, c - 2, first)
                    if stage_a and c in (5, 6):
                        x1_transposes(n + 1, c - 5)
                ffn_out(n, HC - 2)

            gate_block(GATED + 1)
            y_products(0, first=True)
            gate_block(GATED + 2)
            for pair in range(2):
                out_products(0, pair)
            gate_block(GATED + 3)
            for pair in range(2):
                x1_transposes(0, pair)
            pe.wait_ge(s_wt, 4)
            pe.wait_ge(s_scale, 1)
            iteration(0, True, first=True)
            with pe.Fori(1, NB - 1) as i:
                iteration(i, True)
            iteration(NB - 1, False)
            ffn_out(NB - 1, HC - 1)

        @block.vector
        def _(dve):
            def x_out(j, s):
                dve.wait_ge(s_xt, j * STEPS + s + 1)
                nc.vector.tensor_copy(xT[:, j, :, s * P:(s + 1) * P],
                                      bank[s][:, 0:DM].rearrange("p (k r) -> p k r", k=KD)).then_inc(s_xtr, 1)

            def u_out(j, half):
                dve.wait_ge(s_umm, j * 2 + half + 1)
                nc.vector.tensor_scalar(
                    hu[NS:P, bass.ds(j * STEPS + half * 2, 2), :],
                    bank[4 + half][NS:P, 0:N // 2].rearrange("p (s r) -> p s r", r=P),
                    b_in_col[NS:P, :], None, ALU.add).then_inc(s_u, 1)

            dve.wait_ge(s_wa, 64)
            with dve.Fori(0, NB) as j:
                for s in range(STEPS):
                    x_out(j, s)
                for half in range(2):
                    u_out(j, half)
            dve.wait_ge(s_h, WARM)
            nc.vector.tensor_copy(guess, end_state).then_inc(s_guess, 1)

            dve.wait_ge(s_w12, 32)
            nc.vector.tensor_scalar(neg_w1, w1_stage, 0.0, None, ALU.is_lt)
            nc.vector.tensor_scalar(neg_w2, w2_stage, 0.0, None, ALU.is_lt)
            nc.vector.tensor_reduce(alpha1[:, :], w1_stage, AX.X, ALU.add, apply_absolute_value=True)
            nc.vector.tensor_reduce(alpha2[:, :], w2_stage, AX.X, ALU.add, apply_absolute_value=True).then_inc(s_prep, 1)
            dve.wait_ge(s_prep, 1)
            nc.vector.scalar_tensor_tensor(out=w1_sgn, in0=w1_stage, scalar=0.0, in1=neg_w1, op0=ALU.is_gt,
                                           op1=ALU.subtract).then_inc(s_sgn, 1)
            nc.vector.scalar_tensor_tensor(out=w2_sgn, in0=w2_stage, scalar=0.0, in1=neg_w2, op0=ALU.is_gt,
                                           op1=ALU.subtract).then_inc(s_sgn, 1)
            dve.wait_ge(s_const, 3)
            dve.wait_ge(s_wc, 96)
            for k in range(KD):
                nc.vector.tensor_scalar(diag[:, k, :], ident[:, :], alpha2[:, k:k + 1], 1.0 / H, ALU.mult,
                                        ALU.mult).then_inc(s_dg, 1)
            nc.vector.scalar_tensor_tensor(out=abs_b1, in0=b1_col[:, :], scalar=-1.0, in1=b1_col[:, :], op0=ALU.mult,
                                           op1=ALU.max).then_inc(s_prep, 1)
            dve.wait_ge(s_prep, 2)
            nc.vector.tensor_tensor(bound, alpha1[:, :], abs_b1, ALU.add).then_inc(s_prep, 1)
            dve.wait_ge(s_prep, 3)
            nc.vector.tensor_reduce(bound_max, bound, AX.X, ALU.max).then_inc(s_prep, 1)
            nc.vector.tensor_scalar(alpha1[:, :], alpha1[:, :], 1.0 / (DM * X_SCALE), None, ALU.mult).then_inc(s_prep, 1)

            def keep_x(j):
                dve.wait_ge(s_g, j * KD + KD)
                nc.vector.scalar_tensor_tensor(
                    out=xT[:, j].rearrange("p k n -> p (k n)"), in0=gT[:, j].rearrange("p k n -> p (k n)"),
                    scalar=-1.0, in1=xT[:, j].rearrange("p k n -> p (k n)"), op0=ALU.add,
                    op1=ALU.mult).then_inc(s_gx, 1)

            with dve.Fori(0, GATED) as j:
                keep_x(j)

            dve.wait_ge(s_h, WARM + L)
            nc.vector.tensor_tensor(gap, end_state, guess, ALU.subtract).then_inc(s_cmp, 1)
            dve.wait_ge(s_cmp, 1)
            nc.vector.tensor_reduce(gap_max, gap, AX.XY, ALU.max, apply_absolute_value=True).then_inc(s_cmp, 1)
            dve.wait_ge(s_cmp, 2)
            nc.vector.tensor_scalar(gap_flag, gap_max, GUESS_TOLERANCE, None, ALU.is_gt).then_inc(s_cmp, 1)
            dve.wait_ge(s_cdp, 1)
            nc.vector.tensor_copy(cd_t[:, :], bank[1][:, 0:DM]).then_inc(s_cd, 1)
            dve.wait_ge(s_mt, 1)
            nc.vector.tensor_reduce(bound_all, bank[7][0:1, 0:P], AX.X, ALU.max).then_inc(s_m1, 1)
            dve.wait_ge(s_mb, 1)
            nc.vector.tensor_scalar(bound_pow, bank[7][:, 0:1], 2.0 ** -100, None, ALU.max).then_inc(s_prep, 1)
            dve.wait_ge(s_prep, 6)
            nc.vector.tensor_single_scalar(bound_pow.bitcast(I32), bound_pow.bitcast(I32), EXPONENT_BITS,
                                           ALU.bitwise_and).then_inc(s_prep, 1)
            dve.wait_ge(s_prep, 7)
            nc.vector.tensor_scalar(inv_scale, bound_pow, 1.0 / TOP, None, ALU.mult).then_inc(s_prep, 1)
            dve.wait_ge(s_prep, 8)
            nc.vector.reciprocal(hid_scale, inv_scale).then_inc(s_prep, 1)
            dve.wait_ge(s_a2p, 1)
            nc.vector.tensor_scalar(alpha2_row[:, :], bank[0][:, 0:DM], inv_scale, None, ALU.mult).then_inc(s_a2, 1)
            dve.wait_ge(s_cnt, 1)
            nc.vector.tensor_copy(flag_i[:, :], bank[6][0:1, 0:1]).then_inc(s_flag, 1)
            dve.wait_ge(s_flag, 1)
            differ = dve.value_load(flag_i[0:1, 0:1], min_val=0, max_val=NS)
            with dve.If(differ):
                nc.vector.tensor_copy(guess, end_state).then_inc(s_rh, 1)
                with dve.Fori(1, CHUNKS) as r:
                    dve.wait_ge(s_rh, r * (L + 1))
                    nc.vector.tensor_copy(guess, end_state).then_inc(s_rh, 1)
                dve.wait_ge(s_rh, CHUNKS * (L + 1))
            nc.vector.tensor_copy(small[:, 31:32], inv_scale).then_inc(s_done, 1)
            nc.vector.tensor_copy(small[:, 30:31], inv_scale).then_inc(s_scale, 1)

            def gate_y(n, m):
                dve.wait_ge(s_ymm, n * KD + m + 1)
                nc.vector.tensor_tensor(gT[:, n, m, :], bank[6 + m][:, :], gT[:, n, m, :], ALU.mult).then_inc(s_t, 1)

            PER = 9

            def first_sum(n, pair):
                dve.wait_ge(s_omm, n * 2 + pair + 1)
                dve.wait_ge(s_xb, n + 1)
                for e in range(2):
                    t = 2 * pair + e
                    done = nc.vector.scalar_tensor_tensor(out=x1_rows[:, t, :], in0=x1_rows[:, t, :], scalar=2.0,
                                                          in1=bank[6 + pair][:, e * DM:(e + 1) * DM], op0=ALU.mult,
                                                          op1=ALU.add)
                done.then_inc(s_ln, 1)

            def spread(which, rows, tiles):
                for t in tiles:
                    done = nc.vector.bn_stats(stats[:, which, t, :], rows[:, t, :])
                done.then_inc(s_ln, 1)

            def mean_and_variance(which, tiles):
                for t in tiles:
                    done = nc.vector.bn_aggr(moments[:, which, t, :], stats[:, which, t, :])
                done.then_inc(s_ln, 1)

            def add_eps(which, tiles, done_sem):
                lo, hi = tiles[0], tiles[-1] + 1
                nc.vector.tensor_scalar(rstd[:, which, lo:hi], moments[:, which, lo:hi, 1], LN_EPS, None,
                                        ALU.add).then_inc(done_sem, 1)

            def normalise(which, rows, tiles, done_sem):
                for t in tiles:
                    done = nc.vector.tensor_scalar(rows[:, t, :], rows[:, t, :], moments[:, which, t, 0:1],
                                                   rstd[:, which, t:t + 1], ALU.subtract, ALU.mult)
                done.then_inc(done_sem, 1)

            PAIRS = ((0, 1), (2, 3))
            ALL = (0, 1, 2, 3)

            def first_norm(n, pair):
                dve.wait_ge(s_rs1, n * 2 + pair + 1)
                normalise(0, x1_rows, PAIRS[pair], s_x1)

            def second_norm(n):
                dve.wait_ge(s_rs2, n + 1)
                normalise(1, rows_of(gT, n), ALL, s_or)

            def x1_lo(n, pair):
                dve.wait_ge(s_xhi, n * 2 + pair + 1)
                nc.vector.scalar_tensor_tensor(
                    out=x1T[:, n, 1, 2 * pair:2 * pair + 2].rearrange("p s k r -> p (s k r)"),
                    in0=bank[6 + pair][:, :], scalar=X_SCALE,
                    in1=x1T[:, n, 0, 2 * pair:2 * pair + 2].rearrange("p s k r -> p (s k r)"),
                    op0=ALU.mult, op1=ALU.subtract).then_inc(s_xlo, 1)

            def hidden_lo(n, c):
                dve.wait_ge(s_hhi, n * HC + c + 1)
                nc.vector.scalar_tensor_tensor(out=hid[:, c % 4, 1, :], in0=g32[:, c % 2, :],
                                               scalar=hid_scale[:, 0:1], in1=hid[:, c % 4, 0, :], op0=ALU.mult,
                                               op1=ALU.subtract).then_inc(s_hlo, 1)

            def ffn_scale(n):
                dve.wait_ge(s_f2, n * HC + HC)
                for t in range(STEPS):
                    nc.vector.tensor_tensor(fin[:, t, :], bank[t][:, 0:DM], alpha2_row[:, :], ALU.mult).then_inc(s_fin, 1)

            def iteration(n, stage_a, final, store, base):
                link = base
                rows2 = rows_of(gT, n - 1) if final else None
                if stage_a:
                    gate_y(n + 1, 0)
                hidden_lo(n, 0)
                if stage_a:
                    gate_y(n + 1, 1)
                if final:
                    ffn_scale(n - 1)
                if store:
                    second_norm(n - 2)
                hidden_lo(n, 1)
                hidden_lo(n, 2)
                if stage_a:
                    first_sum(n + 1, 0)
                    link += 1
                    dve.wait_ge(s_ln, link)
                    spread(0, x1_rows, PAIRS[0])
                    link += 1
                    spread0 = link
                if final:
                    dve.wait_ge(s_r2, n)
                    if stage_a:
                        dve.wait_ge(s_ln, spread0)
                    spread(1, rows2, PAIRS[0])
                    link += 1
                elif stage_a:
                    dve.wait_ge(s_ln, spread0)
                if stage_a:
                    mean_and_variance(0, PAIRS[0])
                    link += 1
                    dve.wait_ge(s_ln, link)
                    add_eps(0, PAIRS[0], s_v1)
                hidden_lo(n, 3)
                if stage_a:
                    first_sum(n + 1, 1)
                    link += 1
                    sum1 = link
                if final:
                    spread(1, rows2, PAIRS[1])
                    link += 1
                    spread2 = link
                if stage_a:
                    dve.wait_ge(s_ln, sum1)
                    spread(0, x1_rows, PAIRS[1])
                    link += 1
                    spread1 = link
                    first_norm(n + 1, 0)
                    dve.wait_ge(s_ln, spread1)
                if final:
                    dve.wait_ge(s_ln, spread2)
                hidden_lo(n, 4)
                if final:
                    mean_and_variance(1, ALL)
                    link += 1
                    moments2 = link
                if stage_a:
                    mean_and_variance(0, PAIRS[1])
                    link += 1
                    moments1 = link
                if final:
                    dve.wait_ge(s_ln, moments2)
                    add_eps(1, ALL, s_v2)
                if stage_a:
                    dve.wait_ge(s_ln, moments1)
                    add_eps(0, PAIRS[1], s_v1)
                hidden_lo(n, 5)
                if stage_a:
                    first_norm(n + 1, 1)
                    x1_lo(n + 1, 0)
                hidden_lo(n, 6)
                if stage_a:
                    x1_lo(n + 1, 1)
                hidden_lo(n, 7)
                return link

            for m in range(KD):
                gate_y(0, m)
            keep_x(GATED)
            link = 0
            for pair in range(2):
                first_sum(0, pair)
                link += 1
                dve.wait_ge(s_ln, link)
                spread(0, x1_rows, PAIRS[pair])
                link += 1
                dve.wait_ge(s_ln, link)
                mean_and_variance(0, PAIRS[pair])
                link += 1
                dve.wait_ge(s_ln, link)
                add_eps(0, PAIRS[pair], s_v1)
            for pair in range(2):
                first_norm(0, pair)
            for n in range(GATED + 1, NB - 1):
                keep_x(n)
            for pair in range(2):
                x1_lo(0, pair)
            keep_x(NB - 1)
            at = iteration(0, True, False, False, link)
            at = iteration(1, True, True, False, at)
            with dve.Fori(2, NB - 1) as i:
                iteration(i, True, True, True, i * PER + (at - 2 * PER))
            at = iteration(NB - 1, False, True, True, at + (NB - 3) * PER)
            second_norm(NB - 2)
            link = at
            last = rows_of(gT, NB - 1)
            dve.wait_ge(s_f2, NB * HC)
            for tiles in PAIRS:
                for t in tiles:
                    done = nc.vector.tensor_tensor(fin[:, t, :], bank[t][:, 0:DM], alpha2_row[:, :], ALU.mult)
                done.then_inc(s_ln, 1)
                link += 1
                dve.wait_ge(s_ln, link)
                for t in tiles:
                    done = nc.vector.tensor_tensor(last[:, t, :], fin[:, t, :], last[:, t, :], ALU.add)
                done.then_inc(s_ln, 1)
                link += 1
                dve.wait_ge(s_ln, link)
                spread(1, last, tiles)
                link += 1
                dve.wait_ge(s_ln, link)
                mean_and_variance(1, tiles)
                link += 1
                dve.wait_ge(s_ln, link)
                add_eps(1, tiles, s_v2)
            for pair, tiles in enumerate(PAIRS):
                dve.wait_ge(s_rs2, NB + pair)
                normalise(1, last, tiles, s_or)


_INS = ['L0_attn_x', 'L0_attn_W_in', 'L0_attn_b_in', 'L0_attn_W_gate', 'L0_attn_b_gate', 'L0_attn_A', 'L0_attn_Bm',
        'L0_attn_C', 'L0_attn_D', 'L0_attn_W_out', 'L0_attn_b_out', 'L0_ffn_w1', 'L0_ffn_b1', 'L0_ffn_w2', 'L0_ffn_b2']


def kernel(**inputs):
    import numpy as _np
    import concourse.bacc as _bacc
    from concourse import mybir as _mybir
    from concourse.bass_utils import run_bass_kernel_spmd as _run

    nc = _bacc.Bacc("TRN2", target_bir_lowering=False, num_devices=1)
    arrays, args = {}, []
    for name in _INS:
        a = _np.ascontiguousarray(inputs[name])
        arrays[f"in_{name}"] = a
        args.append(nc.dram_tensor(f"in_{name}", a.shape, _mybir.dt.from_np(a.dtype), kind="ExternalInput").ap())
    shape = arrays["in_L0_attn_x"].shape
    args.append(nc.dram_tensor("out_rows", shape, _mybir.dt.float32, kind="ExternalOutput").ap())
    gated_rnn_ffn(nc, *args)
    r = _run(nc, [arrays], core_ids=[0])
    return r.results[0]["out_rows"]
```

```python
from contextlib import ExitStack

import concourse.bass as bass
from concourse import mybir

F32 = mybir.dt.float32
F16 = mybir.dt.float16
F32R = mybir.dt.float32r
I32 = mybir.dt.int32
ALU = mybir.AluOpType
ACT = mybir.ActivationFunctionType
AX = mybir.AxisListType

P = 128
STEPS = 4
RING = 3
WARM = 40
LN_EPS = 1e-5
GUESS_TOLERANCE = 2.0 ** -18
X_SCALE = 1024.0
TOP = 2.0 ** 14
EXPONENT_BITS = 0x7F800000


def gated_rnn_ffn(nc, x, W_in, b_in, W_gate, b_gate, A, Bm, C, D, W_out, b_out, w1, b1, w2, b2, out):
    BATCH, T, DM = x.shape
    NS = A.shape[0]
    H = w1.shape[0]
    KD = DM // P
    HC = H // P
    CHUNKS = P // BATCH
    L = T // CHUNKS
    NB = L // STEPS
    N = STEPS * P
    T0 = L - WARM
    B0 = T0 // STEPS
    LATE = 5
    GATED = NB - LATE
    PREP = 10
    assert NS == 64 and KD == 2 and L % STEPS == 0 and T0 % STEPS == 0 and N == 512 and HC == 8
    assert (NB - 1 - B0) % RING == 0 and GATED == NB - B0 + 1
    assert B0 % 2 == 0 and PREP % 2 == 0 and NB % 2 == 0

    x_rows = x.rearrange("b (c s) d -> (b c) s d", s=L)
    out_rows = out.rearrange("b (c s) d -> (b c) s d", s=L)

    with ExitStack() as ctx:
        def sb(name, shape, dt=F32):
            return ctx.enter_context(nc.sbuf_tensor(name, shape, dt))

        def sem(name):
            return ctx.enter_context(nc.semaphore(name))

        xT = sb("xT", [P, NB, KD, N])
        gT = sb("gT", [P, NB, KD, N])
        hu = sb("hu", [P, L + 1, P])
        with nc.sbuf_tensor("w_in", [P, KD, P], F32) as w_in:
            pass
        cd_lo = sb("cd_lo", [P, DM], F32R)
        w_gate = sb("w_gate", [P, KD, DM])
        w_out_hi = sb("w_out_hi", [P, KD, DM], F32R)
        w_out_lo = sb("w_out_lo", [P, KD, DM], F32R)
        w_rec = sb("w_rec", [P, NS])
        cd_hi = sb("cd_hi", [P, DM], F32R)
        w1s = sb("w1s", [P, KD, H], F16)
        w2s = sb("w2s", [P, HC, DM], F16)
        b_in_col = sb("b_in_col", [P, 1])
        b_gate_col = sb("b_gate_col", [P, KD])
        b1_col = sb("b1_col", [P, HC])
        alpha1 = sb("alpha1", [P, HC])
        alpha2 = sb("alpha2", [P, KD])
        alpha2_row = sb("alpha2_row", [P, DM])
        half_b_out = sb("half_b_out", [P, DM])
        b2_row = sb("b2_row", [P, DM])
        ident = sb("ident", [P, P])
        ident16 = sb("ident16", [P, P], F16)
        small = sb("small", [P, 32])
        neg_half = sb("neg_half", [P, STEPS])
        flag_i = sb("flag_i", [1, 1], I32)
        with nc.sbuf_tensor("xg_hi", [P, 2, KD, N], F32R) as xg_hi, nc.sbuf_tensor("xg_lo", [P, 2, KD, N], F32R) as xg_lo:
            pass
        g32 = sb("g32", [P, 2, N])
        with nc.sbuf_tensor("fin", [P, STEPS, DM], F32) as fin:
            pass
        hu_hi = sb("hu_hi", [P, STEPS, P], F32R)
        hu_lo = sb("hu_lo", [P, STEPS, P], F32R)
        ys_hi = sb("ys_hi", [P, KD, N], F32R)
        with nc.sbuf_tensor("x_load", [P, STEPS, DM], F32) as x_load:
            pass
        ys_lo = sb("ys_lo", [P, KD, N], F32R)
        x1_rows = sb("x1_rows", [P, STEPS, DM])
        with nc.sbuf_tensor("w_gate_hi", [P, KD, DM], F32R) as w_gate_hi, \
                nc.sbuf_tensor("w_gate_lo", [P, KD, DM], F32R) as w_gate_lo:
            pass
        hid = sb("hid", [P, 3, 2, N], F16)
        stats = sb("stats", [P, 2, STEPS, 6])
        moments = sb("moments", [P, 2, STEPS, 2])
        rstd = sb("rstd", [P, 2, STEPS])

        bank = [ctx.enter_context(nc.psum_tensor(f"bank{i}", [P, N], F32)) for i in range(8)]

        s_win = sem("w_in_in")
        s_bin = sem("b_in_in")
        s_wrec = sem("recurrence_weights_in")
        s_wb = sem("gate_weights_in")
        s_wc = sem("late_weights_in")
        s_w12 = sem("ffn_weights_in")
        s_x0 = [sem(f"first_step_in{i}") for i in range(STEPS)]
        s_xin = [sem(f"x_block_in{i}") for i in range(RING)]
        s_const = sem("constants_ready")
        s_ident = sem("identity_steps")
        s_h0 = sem("initial_state_ready")
        s_xt = sem("x_transposed")
        s_xtr = sem("xT_ready")
        s_umm = sem("u_product")
        s_u = sem("u_ready")
        s_scan = sem("scan_product")
        s_h = sem("state_ready")
        s_guess = sem("guess_set")
        s_wgs = sem("w_gate_parts_ready")
        s_xgh = [sem(f"gate_x_hi_ready{i}") for i in range(2)]
        s_xgl = [sem(f"gate_x_parts_ready{i}") for i in range(2)]
        s_gmm = sem("gate_product")
        s_g = sem("gate_ready")
        s_cmp = sem("compare_steps")
        s_cnt = sem("mismatches_counted")
        s_flag = sem("flag_ready")
        s_rscan = sem("repair_product")
        s_rh = sem("repair_state")
        s_done = sem("states_final")
        s_prep = sem("prep_chain")
        s_sgn = sem("signs_ready")
        s_cdp = sem("cd_transposed")
        s_cd = sem("cd_ready")
        s_wtp = sem("signs_transposed")
        s_wt = sem("sign_weights_ready")
        s_mt = sem("bound_transposed")
        s_m1 = sem("bound_reduced")
        s_mb = sem("bound_broadcast")
        s_a2p = sem("alpha2_broadcast")
        s_dg = sem("alpha2_diagonal")
        s_scale = sem("scales_ready")
        s_hb = sem("half_bias_ready")
        s_shift = sem("states_aligned")
        s_huhi = sem("hu_hi_ready")
        s_hulo = sem("hu_lo_ready")
        s_ymm = sem("y_product")
        s_t = sem("gated_y_ready")
        s_ys = sem("ys_ready")
        s_yhi = sem("ys_hi_ready")
        s_ylo = sem("ys_lo_ready")
        s_wsplit = sem("w_out_parts_ready")
        s_omm = sem("out_product")
        s_xl = sem("x_reloaded")
        s_xb = sem("x_plus_bias_ready")
        s_ln = sem("norm_chain")
        s_v1 = sem("first_variance_ready")
        s_rs1 = sem("first_rstd_ready")
        s_v2 = sem("second_variance_ready")
        s_rs2 = sem("second_rstd_ready")
        s_x1 = sem("x1_ready")
        s_x1t = sem("x1_transposed")
        s_xhi = sem("x1_hi_ready")
        s_xlo = sem("x1_lo_ready")
        s_x1b = sem("residual_ready")
        s_f1 = sem("hidden_product")
        s_gelu = sem("gelu_ready")
        s_hhi = sem("hidden_hi_ready")
        s_hlo = sem("hidden_lo_ready")
        s_f2 = sem("ffn_product")
        s_fin = sem("ffn_sum_ready")
        s_r2 = sem("ffn_residual_ready")
        s_or = sem("out_ready")
        s_st = sem("out_stored")

        cd_t = hid[:, 2].rearrange("p a n -> p (a n)").bitcast(F32)[:, 0:DM]
        def xrow_buf(slot):
            return gT[:, slot].rearrange("p k n -> p (k n)").rearrange("p (s d) -> p s d", d=DM)

        def rows_of(buf, n):
            return buf[:, n].rearrange("p k n -> p (k n)").rearrange("p (s d) -> p s d", d=DM)

        x1T = xT[:, :, :, :].rearrange("p b k n -> p b (k n)").bitcast(F16).rearrange(
            "p b (h s k r) -> p b h s k r", h=2, s=STEPS, k=KD)
        STAGED = 4
        w1_stage = gT[:, NB - 2:NB].rearrange("p b k n -> p (b k n)").rearrange("p (j d) -> p j d", d=DM)
        w2_stage = gT[:, NB - STAGED:NB - 2].rearrange("p b k n -> p (b k n)").rearrange("p (k h) -> p k h", k=KD)
        w1_sgn = gT[:, GATED - 3].rearrange("p k n -> p (k n)").bitcast(F16).rearrange("p (j d) -> p j d", d=DM)
        w2_sgn = gT[:, GATED - 1].rearrange("p k n -> p (k n)").bitcast(F16).rearrange("p (k h) -> p k h", k=KD)
        neg_w2 = gT[:, GATED - 2].rearrange("p k n -> p (k n)").bitcast(F16).rearrange("p (k h) -> p k h", k=KD)
        neg_w1 = gT[:, GATED].rearrange("p k n -> p (k n)").bitcast(F16).rearrange("p (j d) -> p j d", d=DM)
        cd_stage = x1_rows[:, 0:1, :].rearrange("p a (k n) -> p (a k) n", k=KD)
        w_out_stage = x1_rows[:, 2:4, :]
        diag = x1_rows[:, 1:2, :].rearrange("p a (k n) -> p (a k) n", k=KD)
        end_state = hu[0:NS, L, :].rearrange("p (b c) -> p b c", b=BATCH)[:, :, 0:CHUNKS - 1]
        guess = hu[0:NS, 0, :].rearrange("p (b c) -> p b c", b=BATCH)[:, :, 1:CHUNKS]
        gap = x1_rows[0:NS, 0, 0:P - BATCH].rearrange("p (b c) -> p b c", b=BATCH)
        ones = x1_rows[:, 2, 0:P]
        gap_max = small[0:NS, 0:1]
        gap_flag = small[0:NS, 1:2]
        bound = small[:, 2:2 + HC]
        bound_max = small[:, 10:11]
        bound_all = small[0:1, 11:12]
        inv_scale = small[:, 12:13]
        hid_scale = small[:, 13:14]
        bound_pow = small[:, 14:15]
        abs_b1 = small[:, 16:16 + HC]

        HALVES = (slice(0, NS), slice(NS, P))
        WHOLE_Y = 3

        def beside(n, half):
            return hu[HALVES[half], bass.ds(n * STEPS + (1 - half), STEPS), :]

        def apart(eng):
            eng.wait_ge(s_const, 3)

        block = ctx.enter_context(nc.Block())

        @block.sync
        def _(sp):
            for s in range(STEPS):
                sp.dma_start(xrow_buf(0)[:, s, :], x_rows[:, T0 + s, :]).then_inc(s_x0[s], 16)
            for o in range(1, RING):
                sp.dma_start(xrow_buf(o), x_rows[:, T0 + o * STEPS:T0 + (o + 1) * STEPS, :]).then_inc(s_xin[o], 16)
            with sp.Fori(0, (NB - 1 - B0) // RING - 1) as i:
                for q in range(RING):
                    sp.wait_ge(s_xt, i * (RING * STEPS) + (q + 1) * STEPS)
                    sp.dma_start(xrow_buf(q), x_rows[:, bass.ds(i * (RING * STEPS) + (T0 + (RING + q) * STEPS), STEPS), :]
                                 ).then_inc(s_xin[q], 16)
            for o in range(NB - B0 - 1, NB):
                block_o = (B0 + o) % NB
                sp.wait_ge(s_xt, (o - RING + 1) * STEPS)
                sp.dma_start(xrow_buf(o % RING), x_rows[:, block_o * STEPS:(block_o + 1) * STEPS, :]
                             ).then_inc(s_xin[o % RING], 16)
            sp.dma_start(w1_stage, w1.rearrange("(p j) d -> p j d", j=HC)).then_inc(s_w12, 16)
            sp.dma_start(w2_stage, w2.rearrange("(k p) h -> p k h", p=P)).then_inc(s_w12, 16)
            sp.wait_ge(s_gmm, (GATED + 1) * KD)
            sp.dma_start(x_load[:, :, :], x_rows[:, 0:STEPS, :]).then_inc(s_xl, 16)
            for n in range(1, 4):
                sp.wait_ge(s_omm, n * 2)
                sp.dma_start(x_load[:, :, :], x_rows[:, n * STEPS:(n + 1) * STEPS, :]).then_inc(s_xl, 16)
            with sp.Fori(0, NB - 4) as i:
                sp.wait_ge(s_or, i + 1)
                sp.dma_start(out_rows[:, bass.ds(i * STEPS, STEPS), :], rows_of(gT, i)).then_inc(s_st, 16)
                sp.wait_ge(s_omm, i * 2 + 8)
                sp.dma_start(x_load[:, :, :], x_rows[:, bass.ds((i + 4) * STEPS, STEPS), :]).then_inc(s_xl, 16)
            for n in range(NB - 4, NB - 1):
                sp.wait_ge(s_or, n + 1)
                sp.dma_start(out_rows[:, n * STEPS:(n + 1) * STEPS, :], rows_of(gT, n)).then_inc(s_st, 16)
            for done, pair in enumerate((1, 0)):
                sp.wait_ge(s_or, NB + done)
                at = L - STEPS + 2 * pair
                sp.dma_start(out_rows[:, at:at + 2, :], rows_of(gT, NB - 1)[:, 2 * pair:2 * pair + 2, :]).then_inc(s_st, 16)
            sp.wait_ge(s_st, 16 * (NB + 1))

        @block.gpsimd
        def _(pool):
            pool.memset(ident[:, :], 0.0).then_inc(s_ident, 1)
            pool.memset(hu[0:NS, 0, :], 0.0).then_inc(s_h0, 1)
            pool.memset(hu[0:NS, T0, :], 0.0).then_inc(s_h, 1)
            pool.memset(w_in[:, :, 0:NS], 0.0).then_inc(s_h0, 1)
            pool.memset(neg_half[:, :], -0.5).then_inc(s_const, 1)
            pool.wait_ge(s_ident, 1)
            pool.affine_select(out=ident[:, :], in_=ident[:, :], compare_op=ALU.not_equal, fill=1.0, base=0,
                               pattern=[[-1, P]], channel_multiplier=1).then_inc(s_const, 1)
            pool.wait_ge(s_const, 2)
            pool.tensor_copy(ident16[:, :], ident[:, :]).then_inc(s_const, 1)
            pool.dma_start(cd_stage[:, :, 0:NS], C.rearrange("(k p) s -> p k s", p=P)).then_inc(s_wc, 16)
            pool.dma_start(cd_stage[:, :, NS:2 * NS], D.rearrange("(k p) s -> p k s", p=P)).then_inc(s_wc, 16)
            pool.dma_start(w_out_stage, W_out.rearrange("(k p) m -> p k m", p=P)).then_inc(s_wc, 16)
            pool.dma_start(b1_col[:, :], b1.rearrange("(p j) -> p j", j=HC)).then_inc(s_wc, 16)
            pool.dma_start(half_b_out[:, :], b_out.partition_broadcast(P)).then_inc(s_wc, 16)
            pool.dma_start(b2_row[:, :], b2.partition_broadcast(P)).then_inc(s_wc, 16)

            pool.wait_ge(s_wb, 32)
            pool.tensor_copy(w_gate_hi[:, :, :], w_gate[:, :, :]).then_inc(s_wgs, 1)
            pool.wait_ge(s_wgs, 1)
            pool.tensor_tensor(w_gate_lo[:, :, :], w_gate[:, :, :], w_gate_hi[:, :, :].bitcast(F32),
                               ALU.subtract).then_inc(s_wgs, 1)

            for n in range(0, GATED, 2):
                pool.wait_ge(s_xgh[0], n // 2 + 1)
                for k in range(KD):
                    pool.tensor_tensor(xg_lo[:, 0, k, :], xT[:, n, k, :], xg_hi[:, 0, k, :].bitcast(F32),
                                       ALU.subtract).then_inc(s_xgl[0], 1)

            def hu_low(n, half):
                apart(pool)
                pool.wait_ge(s_huhi, n * 2 + (half + 1 - 2 * WHOLE_Y))
                pool.tensor_tensor(hu_lo[HALVES[half], :, :], beside(n, half), hu_hi[HALVES[half], :, :].bitcast(F32),
                                   ALU.subtract).then_inc(s_hulo, 1)

            def mix(n):
                for m in range(KD):
                    apart(pool)
                    pool.wait_ge(s_t, n * KD + m + 1)
                    pool.tensor_tensor(gT[:, n, m, :], gT[:, n, m, :], xT[:, n, m, :], ALU.subtract).then_inc(s_ys, 1)

            def add_bias(n):
                apart(pool)
                pool.wait_ge(s_xl, n * 16 + 16)
                pool.tensor_tensor(x1_rows[:, :, :], x_load[:, :, :],
                                   half_b_out[:, None, :].broadcast_to([P, STEPS, DM]), ALU.add).then_inc(s_xb, 1)

            def residual(n):
                apart(pool)
                pool.wait_ge(s_x1, n * 2 + 2)
                pool.tensor_tensor(rows_of(gT, n), x1_rows[:, :, :],
                                   b2_row[:, None, :].broadcast_to([P, STEPS, DM]), ALU.add).then_inc(s_x1b, 1)

            def second_sum(n):
                apart(pool)
                pool.wait_ge(s_fin, n * 2 + 2)
                pool.wait_ge(s_x1b, n + 1)
                pool.tensor_tensor(rows_of(gT, n), fin[:, :, :], rows_of(gT, n), ALU.add).then_inc(s_r2, 1)

            def first_rstd(n, pair):
                apart(pool)
                pool.wait_ge(s_v1, n * 2 + pair + 1)
                pool.tensor_tensor(rstd[:, 0, 2 * pair:2 * pair + 2], rstd[:, 0, 2 * pair:2 * pair + 2],
                                   neg_half[:, 0:2], ALU.pow).then_inc(s_rs1, 1)

            def second_rstd(n):
                apart(pool)
                pool.wait_ge(s_v2, n + 1)
                pool.tensor_tensor(rstd[:, 1, :], rstd[:, 1, :], neg_half[:, :], ALU.pow).then_inc(s_rs2, 1)

            def iteration(n, stage_y, stage_a, final, split_next=False):
                if stage_y:
                    mix(n + 2)
                if final:
                    second_sum(n - 1)
                if split_next:
                    hu_low(n + 3, 0)
                if stage_a:
                    first_rstd(n + 1, 0)
                if split_next:
                    apart(pool)
                    pool.wait_ge(s_rs1, n * 2 + 3)
                    hu_low(n + 3, 1)
                    apart(pool)
                    pool.wait_ge(s_hulo, n * 2 + 2)
                if stage_a:
                    first_rstd(n + 1, 1)
                    residual(n + 1)
                if final:
                    second_rstd(n - 1)
                if stage_y:
                    apart(pool)
                    pool.wait_ge(s_x1t, n * 2 + 4)
                    pool.wait_ge(s_x1b, n + 2)
                    add_bias(n + 2)

            pool.wait_ge(s_const, 3)
            pool.wait_ge(s_done, 1)
            pool.wait_ge(s_hb, 1)
            add_bias(0)
            mix(0)
            for pair in range(2):
                first_rstd(0, pair)
            mix(1)
            pool.wait_ge(s_x1t, 2)
            pool.wait_ge(s_x1b, 1)
            add_bias(1)
            iteration(0, True, True, False, split_next=True)
            with pool.Fori(1, NB - 3) as i:
                iteration(i, True, True, True, split_next=True)
            iteration(NB - 3, True, True, True)
            iteration(NB - 2, False, True, True)
            iteration(NB - 1, False, False, True)
            pool.wait_ge(s_fin, NB * 2 - 1)
            pool.wait_ge(s_x1b, NB)
            last = rows_of(gT, NB - 1)
            pool.tensor_tensor(last[:, 0:2, :], fin[:, 0:2, :], last[:, 0:2, :], ALU.add).then_inc(s_r2, 1)
            for done, pair in enumerate((1, 0)):
                tiles = slice(2 * pair, 2 * pair + 2)
                pool.wait_ge(s_v2, NB + done)
                pool.tensor_tensor(rstd[:, 1, tiles], rstd[:, 1, tiles], neg_half[:, 0:2], ALU.pow).then_inc(s_rs2, 1)

        @block.scalar
        def _(act):
            act.dma_start(w_in[:, :, NS:P], W_in.rearrange("(k p) s -> p k s", p=P)).then_inc(s_win, 16)
            act.dma_start(b_in_col[NS:P, :], b_in.rearrange("(s a) -> s a", a=1)).then_inc(s_bin, 16)
            act.dma_start(w_rec[0:NS, :], A).then_inc(s_wrec, 16)
            act.dma_start(w_rec[NS:P, :], Bm).then_inc(s_wrec, 16)
            act.dma_start(w_gate[:, :, :], W_gate.rearrange("(k p) m -> p k m", p=P)).then_inc(s_wb, 16)
            act.dma_start(b_gate_col[:, :], b_gate.rearrange("(k p) -> p k", p=P),
                          allow_slow_non_contiguous=True).then_inc(s_wb, 16)

            act.wait_ge(s_const, 3)
            nc.scalar.activation(small[0:1, 28:29], ident[0:1, 0:1], ACT.Sigmoid)
            with act.Fori(B0, NB) as j:
                for s in range(STEPS):
                    act.wait_ge(s_scan, j * STEPS + (s + 1 - T0))
                    nc.scalar.activation(hu[0:NS, bass.ds(j * STEPS + s + 1, 1), :],
                                         bank[6 + s % 2][0:NS, None, 0:P], ACT.Tanh).then_inc(s_h, 1)

            def gate(j, m):
                act.wait_ge(s_gmm, j * KD + m + 1)
                nc.scalar.activation(gT[:, j, m, :], bank[m][:, :], ACT.Sigmoid,
                                     bias=b_gate_col[:, m:m + 1]).then_inc(s_g, 1)

            def sweep1_block(j, second, first):
                for s in range(STEPS):
                    act.wait_ge(s_scan, j * STEPS + (WARM + s + 1))
                    nc.scalar.activation(hu[0:NS, bass.ds(j * STEPS + s + 1, 1), :],
                                         bank[6 + s % 2][0:NS, None, 0:P], ACT.Tanh).then_inc(s_h, 1)
                    if s == 0 and second is not None:
                        gate(second, 1)
                    if s == 2 and first is not None:
                        gate(first, 0)

            act.wait_ge(s_wb, 32)
            with act.Fori(0, B0 - 1) as j:
                sweep1_block(j, None, None)
            sweep1_block(B0 - 1, None, 0)
            with act.Fori(B0, NB) as j:
                sweep1_block(j, j - B0, j - (B0 - 1))
            gate(GATED - 1, 1)
            act.wait_ge(s_sgn, 2)
            for n in (GATED, GATED + 1):
                for m in range(KD):
                    gate(n, m)
            act.wait_ge(s_flag, 1)
            differ = act.value_load(flag_i[0:1, 0:1], min_val=0, max_val=NS)
            with act.If(differ):
                with act.Fori(0, CHUNKS) as r:
                    with act.Fori(0, L // 2) as j:
                        for s in range(2):
                            act.wait_ge(s_rscan, r * L + j * 2 + s + 1)
                            nc.scalar.activation(hu[0:NS, bass.ds(j * 2 + s + 1, 1), :],
                                                 bank[6 + s][0:NS, None, 0:P], ACT.Tanh).then_inc(s_rh, 1)

            def ys_high(n, m, first=False):
                act.wait_ge(s_ys, n * KD + m + 1)
                if m == 0 and not first:
                    act.wait_ge(s_omm, n * 2)
                nc.scalar.activation(ys_hi[:, m, :], gT[:, n, m, :], ACT.Copy).then_inc(s_yhi, 1)

            def x1_hi(n, pair):
                act.wait_ge(s_x1t, n * 2 + pair + 1)
                nc.scalar.activation(
                    x1T[:, n, 0, 2 * pair:2 * pair + 2].rearrange("p s k r -> p (s k r)"),
                    bank[6 + pair][:, :], ACT.Copy, scale=X_SCALE).then_inc(s_xhi, 1)

            def hu_high(n, half, first):
                if half == 0 and not first:
                    act.wait_ge(s_r2, n - 3)
                nc.scalar.activation(hu_hi[HALVES[half], :, :], beside(n, half), ACT.Copy).then_inc(s_huhi, 1)

            def iteration(n, stage_y, stage_a, split_next=False, first=False):
                for c in range(HC):
                    act.wait_ge(s_f1, n * HC + c + 1)
                    if not (first and c < 2):
                        act.wait_ge(s_hlo, n * HC + c - 1)
                    nc.scalar.activation(g32[:, c % 2, :], bank[4 + c % 2][:, :], ACT.Gelu, bias=b1_col[:, c:c + 1],
                                         scale=alpha1[:, c:c + 1]).then_inc(s_gelu, 1)
                    act.wait_ge(s_gelu, n * HC + c + 1)
                    if not (first and c < 3):
                        act.wait_ge(s_f2, n * HC + c - 2 if c >= 3 else n * HC + (-1, 0, 0)[c])
                    nc.scalar.activation(hid[:, c % 3, 0, :], g32[:, c % 2, :], ACT.Copy,
                                         scale=hid_scale[:, 0:1]).then_inc(s_hhi, 1)
                    if split_next and c in (2, 3):
                        if c == 2 and not first:
                            act.wait_ge(s_ymm, n * KD + 3 * KD)
                        hu_high(n + 3, c - 2, first)
                    if stage_a and c in (5, 6):
                        x1_hi(n + 1, c - 5)
                if stage_y:
                    for m in range(KD):
                        ys_high(n + 2, m)

            for n in range(GATED + 2, NB):
                for m in range(KD):
                    gate(n, m)
                if n == GATED + 2:
                    for m in range(KD):
                        ys_high(0, m, first=True)
            for pair in range(2):
                x1_hi(0, pair)
            nc.scalar.activation(small[0:1, 29:30], ident[0:1, 0:1], ACT.Gelu)
            for m in range(KD):
                ys_high(1, m)
            act.wait_ge(s_scale, 1)
            iteration(0, True, True, split_next=True, first=True)
            with act.Fori(1, NB - 3) as i:
                iteration(i, True, True, split_next=True)
            iteration(NB - 3, True, True)
            iteration(NB - 2, False, True)
            iteration(NB - 1, False, False)

        @block.tensor
        def _(pe):
            def transpose_step(o, s, slot):
                for k in range(KD):
                    done = nc.tensor.transpose(bank[s][:, k * P:(k + 1) * P],
                                               xrow_buf(slot)[:, s, k * P:(k + 1) * P], ident[:, :])
                done.then_inc(s_xt, 1)

            def u_part(o, j, half, k):
                if k == 0:
                    pe.wait_ge(s_xtr, o * STEPS + 2 * half + 2)
                done = nc.tensor.matmul(bank[4 + half][:, 0:N // 2], w_in[:, k, :],
                                        xT[:, j, k, half * (N // 2):(half + 1) * (N // 2)],
                                        start=(k == 0), stop=(k == KD - 1))
                if k == KD - 1:
                    done.then_inc(s_umm, 1)

            def scan_step(t, parity, done_sem):
                nc.tensor.matmul(bank[6 + parity][0:NS, 0:P], w_rec[:, :], hu[:, t, :],
                                 start=True, stop=True).then_inc(done_sem, 1)

            def arrived(o):
                return 16 * (o // RING + (1 if o % RING else 0))

            def feed(s, o, j, nxt=None, slot=None, slot2=None, loads2=0):
                if s == 0:
                    u_part(o, j, 1, 1)
                    if nxt is not None:
                        transpose_step(o + 1, 2, slot)
                if nxt is None:
                    return
                if s == 1:
                    transpose_step(o + 1, 3, slot)
                    u_part(o + 1, nxt, 0, 0)
                if s == 2:
                    u_part(o + 1, nxt, 0, 1)
                if s == 3:
                    u_part(o + 1, nxt, 1, 0)
                if s >= 2 and slot2 is not None:
                    if s == 2:
                        pe.wait_ge(s_xin[slot2], loads2)
                    transpose_step(o + 2, s - 2, slot2)

            def keep_warm(products):
                for i in range(products):
                    nc.tensor.matmul(bank[7][:, 0:P], hu[0:NS, 0, :], hu[0:NS, 0, :], start=True, stop=True)

            pe.wait_ge(s_h0, 1)
            keep_warm(6)

            pe.wait_ge(s_const, 2)
            for half in range(2):
                for s in (2 * half, 2 * half + 1):
                    pe.wait_ge(s_x0[s], 16)
                    transpose_step(0, s, 0)
                    keep_warm(1)
                keep_warm(1)
                if half == 0:
                    pe.wait_ge(s_win, 16)
                    pe.wait_ge(s_h0, 2)
                for k in range(KD):
                    if half == 0 or k == 0:
                        u_part(0, B0, half, k)
            pe.wait_ge(s_xin[1], arrived(1))
            pe.wait_ge(s_xtr, 2)
            for s in range(2):
                transpose_step(1, s, 1)

            pe.wait_ge(s_wrec, 32)

            def sweep0_block(o, q, nxt, loads2):
                j = o + B0
                for s in range(STEPS):
                    if s % 2 == 0:
                        pe.wait_ge(s_u, o * 2 + s // 2 + 1)
                    pe.wait_ge(s_h, o * STEPS + s + 1)
                    scan_step(j * STEPS + s, s % 2, s_scan)
                    feed(s, o, j, nxt, (q + 1) % RING, (q + 2) % RING, loads2)

            with pe.Fori(0, (NB - 1 - B0) // RING) as i:
                for q in range(RING):
                    sweep0_block(i * RING + q, q, i * RING + (q + 1 + B0), i * 16 + arrived(q + 2))
            sweep0_block(NB - 1 - B0, (NB - 1 - B0) % RING, 0, arrived(NB - 1 - B0 + 2))

            def gate_product(j, m, k):
                if k == 0:
                    pe.wait_ge(s_g, j * KD - KD + m + 1)
                done = nc.tensor.matmul(bank[m][:, :], w_gate[:, k, m * P:(m + 1) * P], xT[:, j, k, :],
                                        start=(k == 0), stop=(k == KD - 1))
                if k == KD - 1:
                    done.then_inc(s_gmm, 1)

            def gate_parts(j, slot, m, k, first=False):
                if k == 0 and not first:
                    pe.wait_ge(s_g, j * KD - KD + m + 1)
                if m == 0:
                    pe.wait_ge(s_xgl[slot], (j - slot) + k + 1)
                cols = slice(m * P, (m + 1) * P)
                parts = ((w_gate_hi, xg_hi), (w_gate_lo, xg_hi), (w_gate_hi, xg_lo))
                for i, (w, xg) in enumerate(parts):
                    done = nc.tensor.matmul(bank[m][:, :], w[:, k, cols], xg[:, slot, k, :],
                                            start=(k == 0 and i == 0), stop=(k == KD - 1 and i == len(parts) - 1))
                if k == KD - 1:
                    done.then_inc(s_gmm, 1)

            def gate_block(j, product, *slot):
                for m in range(KD):
                    for k in range(KD):
                        product(j, *slot, m, k)

            pe.wait_ge(s_guess, 1)

            def sweep1_step(j, s):
                pe.wait_ge(s_h, j * STEPS + (1 + WARM + s))
                scan_step(j * STEPS + s, s % 2, s_scan)

            for j in range(B0 - 1):
                o = NB - B0 + 1 + j
                for s in range(STEPS):
                    if s % 2 == 0:
                        pe.wait_ge(s_u, (o - 1) * 2 + s // 2 + 1)
                    sweep1_step(j, s)
                    feed(s, o - 1, j, j + 1, o % RING, (o + 1) % RING if o + 1 < NB else None, arrived(o + 1))
            pe.wait_ge(s_wgs, 2)
            for s in range(STEPS):
                if s % 2 == 0:
                    pe.wait_ge(s_u, (NB - 1) * 2 + s // 2 + 1)
                sweep1_step(B0 - 1, s)
                feed(s, NB - 1, B0 - 1)
                gate_parts(0, 0, s // 2, s % 2, first=True)

            def gated_block(j, slot, beside=None):
                for s in range(STEPS):
                    sweep1_step(j, s)
                    gate_parts(j - (B0 - 1), slot, s // 2, s % 2)
                    if beside is not None:
                        beside(s)

            def prepare_signs(s):
                if s == 0:
                    pe.wait_ge(s_sgn, 2)
                    for k in range(KD):
                        for j in range(HC):
                            done = nc.tensor.transpose(bank[2 + k][:, :].bitcast(F16)[:, j * P:(j + 1) * P],
                                                       w1_sgn[:, j, k * P:(k + 1) * P], ident16[:, :])
                        done.then_inc(s_wtp, 1)
                if s == 1:
                    for j in range(HC):
                        for k in range(KD):
                            at = (j % 4) * DM + k * P
                            done = nc.tensor.transpose(bank[4 + j // 4][:, :].bitcast(F16)[:, at:at + P],
                                                       w2_sgn[:, k, :].rearrange("p (q j) -> p q j", j=HC)[:, :, j],
                                                       ident16[:, :])
                        if j % 4 == 3:
                            done.then_inc(s_wtp, 1)

            def prepare_rows(s):
                if s == 0:
                    pe.wait_ge(s_wc, 96)
                    pe.wait_ge(s_wt, 1)
                    for k in range(KD):
                        done = nc.tensor.transpose(bank[2][:, k * P:(k + 1) * P], cd_stage[:, k, :], ident[:, :])
                    done.then_inc(s_cdp, 1)
                    pe.wait_ge(s_dg, 2)
                    pe.wait_ge(s_wt, 2)
                    for k in range(KD):
                        done = nc.tensor.matmul(bank[3][:, k * P:(k + 1) * P], ones, diag[:, k, :], start=True, stop=True)
                    done.then_inc(s_a2p, 1)
                    pe.wait_ge(s_prep, 4)
                    pe.wait_ge(s_wt, 3)
                    nc.tensor.transpose(bank[4][0:1, 0:P], bound_max, ident[:, :]).then_inc(s_mt, 1)
                if s == 2:
                    pe.wait_ge(s_m1, 1)
                    pe.wait_ge(s_wt, 4)
                    nc.tensor.matmul(bank[5][:, 0:1], ones[0:1, :], bound_all, start=True,
                                     stop=True).then_inc(s_mb, 1)

            with pe.Fori(0, (PREP - B0) // 2) as i:
                for q in range(2):
                    gated_block(i * 2 + (B0 + q), 1 - q)
            gated_block(PREP, 1, prepare_signs)
            gated_block(PREP + 1, 0, prepare_rows)
            with pe.Fori(0, (NB - PREP - 2) // 2) as i:
                for q in range(2):
                    gated_block(i * 2 + (PREP + 2 + q), 1 - q)

            gate_block(GATED, gate_parts, 1)
            pe.wait_ge(s_cmp, 3)
            nc.tensor.matmul(bank[6][0:1, 0:1], gap_flag, ones[0:NS, 0:1], start=True, stop=True).then_inc(s_cnt, 1)
            gate_block(GATED + 1, gate_product)
            pe.wait_ge(s_flag, 1)
            differ = pe.value_load(flag_i[0:1, 0:1], min_val=0, max_val=NS)
            with pe.If(differ):
                with pe.Fori(0, CHUNKS) as r:
                    with pe.Fori(0, L // 2) as j:
                        for s in range(2):
                            pe.wait_ge(s_rh, r * (L + 1) + j * 2 + s + 1)
                            scan_step(j * 2 + s, s, s_rscan)

            def whole_y_products(n):
                pe.wait_ge(s_shift, n * STEPS + STEPS)
                for m in range(KD):
                    if n > 0:
                        pe.wait_ge(s_t, n * KD - KD + m + 1)
                    nc.tensor.matmul(bank[2 + m][:, :], cd_t[:, m * P:(m + 1) * P],
                                     hu[:, bass.ds(n * STEPS, STEPS), :].rearrange("p s r -> p (s r)"),
                                     start=True, stop=True).then_inc(s_ymm, 1)

            def y_products(n):
                pe.wait_ge(s_hulo, n * 2 + (2 - 2 * WHOLE_Y))
                for m in range(KD):
                    pe.wait_ge(s_t, n * KD - KD + m + 1)
                    cols = slice(m * P, (m + 1) * P)
                    parts = ((cd_hi, hu_hi), (cd_lo, hu_hi), (cd_hi, hu_lo))
                    for i, (w, rows) in enumerate(parts):
                        done = nc.tensor.matmul(bank[2 + m][:, :], w[:, cols], rows[:, :, :].rearrange("p s r -> p (s r)"),
                                                start=(i == 0), stop=(i == len(parts) - 1))
                    done.then_inc(s_ymm, 1)

            def out_products(n, pair, first=False):
                pe.wait_ge(s_ylo, n * KD + KD)
                if not first:
                    pe.wait_ge(s_xlo, n * 2 - 1 + pair)
                for e in range(2):
                    tile = 2 * pair + e
                    rows = slice(tile * P, (tile + 1) * P)
                    parts = [(ys, w, k) for k in range(KD)
                             for ys, w in ((ys_hi[:, k, rows], w_out_hi), (ys_hi[:, k, rows], w_out_lo),
                                           (ys_lo[:, k, rows], w_out_hi))]
                    for i, (ys, w, k) in enumerate(parts):
                        done = nc.tensor.matmul(bank[6 + pair][:, e * DM:(e + 1) * DM], ys, w[:, k, :],
                                                start=(i == 0), stop=(i == len(parts) - 1))
                done.then_inc(s_omm, 1)

            def x1_transposes(n, pair):
                pe.wait_ge(s_x1, n * 2 + pair + 1)
                for e in range(2):
                    for k in range(KD):
                        at = (e * KD + k) * P
                        done = nc.tensor.transpose(bank[6 + pair][:, at:at + P],
                                                   x1_rows[:, 2 * pair + e, k * P:(k + 1) * P], ident[:, :])
                done.then_inc(s_x1t, 1)

            def hidden(n, c, first=False):
                if c == 0:
                    pe.wait_ge(s_xlo, n * 2 + 2)
                if not (first and c < 2):
                    pe.wait_ge(s_gelu, n * HC + c - 1)
                for k in range(KD):
                    for part in range(2):
                        done = nc.tensor.matmul(bank[4 + c % 2][:, :], w1s[:, k, c * P:(c + 1) * P],
                                                x1T[:, n, part, :, k, :],
                                                start=(k == 0 and part == 0), stop=(k == KD - 1 and part == 1))
                done.then_inc(s_f1, 1)

            def ffn_out(n, c, first=False):
                pe.wait_ge(s_hlo, n * HC + c + 1)
                for tile in range(STEPS):
                    if c == 0 and not first and tile % 2 == 0:
                        pe.wait_ge(s_fin, n * 2 - 1 + tile // 2)
                    for part in range(2):
                        done = nc.tensor.matmul(bank[tile // 2][:, tile % 2 * DM:(tile % 2 + 1) * DM],
                                                hid[:, c % 3, part, tile * P:(tile + 1) * P],
                                                w2s[:, c, :], start=(c == 0 and part == 0 and tile % 2 == 0),
                                                stop=(c == HC - 1 and part == 1 and tile % 2 == 1))
                done.then_inc(s_f2, 1)

            def iteration(n, stage_y, stage_a, first=False):
                for c in range(HC):
                    hidden(n, c, first)
                    if c == 0:
                        if stage_y and not first:
                            y_products(n + 2)
                        if not first:
                            ffn_out(n - 1, HC - 1)
                    after = 2 if first else 1
                    if stage_a and c in (after, after + 1):
                        out_products(n + 1, c - after)
                    if c >= 2:
                        ffn_out(n, c - 2, first)
                    if stage_a and c in (5, 6):
                        x1_transposes(n + 1, c - 5)
                ffn_out(n, HC - 2)

            pe.wait_ge(s_wsplit, 2)
            whole_y_products(0)
            gate_block(GATED + 2, gate_product)
            gate_block(GATED + 3, gate_product)
            for pair in range(2):
                out_products(0, pair, first=True)
            whole_y_products(1)
            gate_block(GATED + 4, gate_product)
            for pair in range(2):
                x1_transposes(0, pair)
            whole_y_products(2)
            pe.wait_ge(s_wt, 4)
            pe.wait_ge(s_scale, 1)
            iteration(0, True, True, first=True)
            with pe.Fori(1, NB - 2) as i:
                iteration(i, True, True)
            iteration(NB - 2, False, True)
            iteration(NB - 1, False, False)
            ffn_out(NB - 1, HC - 1)

        @block.vector
        def _(dve):
            def x_out(o, j, s):
                dve.wait_ge(s_xt, o * STEPS + s + 1)
                nc.vector.tensor_copy(xT[:, j, :, s * P:(s + 1) * P],
                                      bank[s][:, 0:DM].rearrange("p (k r) -> p k r", k=KD)).then_inc(s_xtr, 1)

            def u_out(o, j, half):
                dve.wait_ge(s_umm, o * 2 + half + 1)
                nc.vector.tensor_scalar(
                    hu[NS:P, bass.ds(j * STEPS + half * 2, 2), :],
                    bank[4 + half][NS:P, 0:N // 2].rearrange("p (s r) -> p s r", r=P),
                    b_in_col[NS:P, :], None, ALU.add).then_inc(s_u, 1)

            def heads(o, j):
                for s in range(2):
                    x_out(o, j, s)

            def rest(o, j, before):
                u_out(o - 1, before, 1)
                for s in range(2, STEPS):
                    x_out(o, j, s)
                u_out(o, j, 0)

            def gate_x_hi(n):
                slot = n % 2
                if n > 1:
                    dve.wait_ge(s_gmm, n * KD - KD)
                nc.vector.tensor_copy(xg_hi[:, slot, :, :], xT[:, n, :, :]).then_inc(s_xgh[slot], 1)

            def gate_x_lo(n):
                dve.wait_ge(s_xgh[1], (n + 1) // 2)
                nc.vector.tensor_tensor(xg_lo[:, 1, :, :], xT[:, n, :, :], xg_hi[:, 1, :, :].bitcast(F32),
                                        ALU.subtract).then_inc(s_xgl[1], KD)

            heads(0, B0)
            dve.wait_ge(s_bin, 16)
            u_out(0, B0, 0)
            for s in range(2, STEPS):
                x_out(0, B0, s)
            with dve.Fori(0, (NB - 1 - B0) // RING) as i:
                for q in range(1, RING + 1):
                    heads(i * RING + q, i * RING + (B0 + q))
                    rest(i * RING + q, i * RING + (B0 + q), i * RING + (B0 + q - 1))
            heads(NB - B0, 0)
            rest(NB - B0, 0, NB - 1)
            heads(NB - B0 + 1, 1)
            dve.wait_ge(s_h, 1 + WARM)
            nc.vector.tensor_copy(guess, end_state).then_inc(s_guess, 1)
            for j in range(1, B0):
                rest(NB - B0 + j, j, j - 1)
                if j + 1 < B0:
                    heads(NB - B0 + j + 1, j + 1)
                if j in (2, 3):
                    gate_x_hi(j - 2)
            u_out(NB - 1, B0 - 1, 1)
            gate_x_lo(1)

            dve.wait_ge(s_w12, 32)
            nc.vector.tensor_scalar(neg_w1[:, :, :], w1_stage, 0.0, None, ALU.is_lt)
            nc.vector.tensor_scalar(neg_w2, w2_stage, 0.0, None, ALU.is_lt)
            gate_x_hi(2)
            nc.vector.tensor_reduce(alpha1[:, :], w1_stage, AX.X, ALU.add, apply_absolute_value=True)
            nc.vector.tensor_reduce(alpha2[:, :], w2_stage, AX.X, ALU.add, apply_absolute_value=True).then_inc(s_prep, 1)
            gate_x_hi(3)
            gate_x_lo(3)
            dve.wait_ge(s_prep, 1)
            gate_x_hi(4)
            nc.vector.scalar_tensor_tensor(out=w1_sgn, in0=w1_stage, scalar=0.0, in1=neg_w1[:, :, :], op0=ALU.is_gt,
                                           op1=ALU.subtract).then_inc(s_sgn, 1)
            nc.vector.scalar_tensor_tensor(out=w2_sgn, in0=w2_stage, scalar=0.0, in1=neg_w2, op0=ALU.is_gt,
                                           op1=ALU.subtract).then_inc(s_sgn, 1)
            gate_x_hi(5)
            gate_x_lo(5)
            dve.wait_ge(s_wc, 96)
            nc.vector.tensor_copy(w_out_hi[:, :, :], w_out_stage).then_inc(s_wsplit, 1)
            dve.wait_ge(s_wsplit, 1)
            nc.vector.tensor_tensor(w_out_lo[:, :, :], w_out_stage, w_out_hi[:, :, :].bitcast(F32),
                                    ALU.subtract).then_inc(s_wsplit, 1)
            dve.wait_ge(s_wsplit, 2)
            nc.vector.memset(ones, 1.0)
            dve.wait_ge(s_const, 3)
            for k in range(KD):
                nc.vector.tensor_scalar(diag[:, k, :], ident[:, :], alpha2[:, k:k + 1], 1.0 / H, ALU.mult,
                                        ALU.mult).then_inc(s_dg, 1)
            nc.vector.scalar_tensor_tensor(out=abs_b1, in0=b1_col[:, :], scalar=-1.0, in1=b1_col[:, :], op0=ALU.mult,
                                           op1=ALU.max).then_inc(s_prep, 1)
            dve.wait_ge(s_prep, 2)
            nc.vector.tensor_tensor(bound, alpha1[:, :], abs_b1, ALU.add).then_inc(s_prep, 1)
            dve.wait_ge(s_prep, 3)
            nc.vector.tensor_reduce(bound_max, bound, AX.X, ALU.max).then_inc(s_prep, 1)
            nc.vector.tensor_scalar(alpha1[:, :], alpha1[:, :], 1.0 / (DM * X_SCALE), None, ALU.mult).then_inc(s_prep, 1)

            gate_x_hi(6)

            def keep_x(j):
                dve.wait_ge(s_g, j * KD + KD)
                nc.vector.scalar_tensor_tensor(
                    out=xT[:, j].rearrange("p k n -> p (k n)"), in0=gT[:, j].rearrange("p k n -> p (k n)"),
                    scalar=-1.0, in1=xT[:, j].rearrange("p k n -> p (k n)"), op0=ALU.add,
                    op1=ALU.mult)

            for w in range(4):
                dve.wait_ge(s_wtp, w + 1)
                src = bank[2 + w][:, :].bitcast(F16)
                if w < 2:
                    nc.vector.tensor_copy(w1s[:, w, :], src).then_inc(s_wt, 1)
                else:
                    nc.vector.tensor_copy(w2s[:, (w - 2) * 4:(w - 1) * 4, :].rearrange("p j d -> p (j d)"),
                                          src).then_inc(s_wt, 1)
            nc.vector.tensor_scalar(half_b_out[:, :], half_b_out[:, :], 0.5, None, ALU.mult).then_inc(s_hb, 1)
            dve.wait_ge(s_cdp, 1)
            nc.vector.tensor_copy(cd_t, bank[2][:, 0:DM]).then_inc(s_cd, 1)
            nc.vector.tensor_copy(cd_hi[:, :], bank[2][:, 0:DM]).then_inc(s_cd, 1)
            dve.wait_ge(s_cd, 2)
            nc.vector.tensor_tensor(cd_lo[:, :], bank[2][:, 0:DM], cd_hi[:, :].bitcast(F32), ALU.subtract).then_inc(s_cd, 1)
            dve.wait_ge(s_mt, 1)
            nc.vector.tensor_reduce(bound_all, bank[4][0:1, 0:P], AX.X, ALU.max).then_inc(s_m1, 1)
            gate_x_hi(7)
            gate_x_lo(7)
            dve.wait_ge(s_mb, 1)
            nc.vector.tensor_scalar(bound_pow, bank[5][:, 0:1], 2.0 ** -100, None, ALU.max).then_inc(s_prep, 1)
            dve.wait_ge(s_prep, 6)
            nc.vector.tensor_single_scalar(bound_pow.bitcast(I32), bound_pow.bitcast(I32), EXPONENT_BITS,
                                           ALU.bitwise_and).then_inc(s_prep, 1)
            dve.wait_ge(s_prep, 7)
            nc.vector.tensor_scalar(inv_scale, bound_pow, 1.0 / TOP, None, ALU.mult).then_inc(s_prep, 1)
            dve.wait_ge(s_prep, 8)
            nc.vector.reciprocal(hid_scale, inv_scale).then_inc(s_prep, 1)
            dve.wait_ge(s_a2p, 1)
            nc.vector.tensor_scalar(alpha2_row[:, :], bank[3][:, 0:DM], inv_scale, None, ALU.mult)
            gate_x_hi(8)
            with dve.Fori(0, 4) as j:
                keep_x(j)
            gate_x_hi(9)
            gate_x_lo(9)
            keep_x(4)
            gate_x_hi(10)
            with dve.Fori(5, GATED - 3) as j:
                keep_x(j)
            gate_x_hi(11)
            gate_x_lo(11)
            with dve.Fori(GATED - 3, GATED - 1) as j:
                keep_x(j)

            dve.wait_ge(s_h, 1 + WARM + L)
            nc.vector.tensor_tensor(gap, end_state, guess, ALU.subtract).then_inc(s_cmp, 1)
            dve.wait_ge(s_cmp, 1)
            nc.vector.tensor_reduce(gap_max, gap, AX.XY, ALU.max, apply_absolute_value=True).then_inc(s_cmp, 1)
            dve.wait_ge(s_cmp, 2)
            nc.vector.tensor_scalar(gap_flag, gap_max, GUESS_TOLERANCE, None, ALU.is_gt).then_inc(s_cmp, 1)
            dve.wait_ge(s_cnt, 1)
            nc.vector.tensor_copy(flag_i[:, :], bank[6][0:1, 0:1]).then_inc(s_flag, 1)
            dve.wait_ge(s_flag, 1)
            differ = dve.value_load(flag_i[0:1, 0:1], min_val=0, max_val=NS)
            with dve.If(differ):
                nc.vector.tensor_copy(guess, end_state).then_inc(s_rh, 1)
                with dve.Fori(1, CHUNKS) as r:
                    dve.wait_ge(s_rh, r * (L + 1))
                    nc.vector.tensor_copy(guess, end_state).then_inc(s_rh, 1)
                dve.wait_ge(s_rh, CHUNKS * (L + 1))
            nc.vector.tensor_copy(small[:, 31:32], inv_scale).then_inc(s_done, 1)
            nc.vector.tensor_copy(small[:, 30:31], inv_scale).then_inc(s_scale, 1)

            def gate_y(n, m):
                dve.wait_ge(s_ymm, n * KD + m + 1)
                nc.vector.tensor_tensor(gT[:, n, m, :], bank[2 + m][:, :], gT[:, n, m, :], ALU.mult).then_inc(s_t, 1)

            def ys_low(n, m):
                dve.wait_ge(s_yhi, n * KD + m + 1)
                dve.wait_ge(s_xb, n + 1)
                nc.vector.tensor_tensor(ys_lo[:, m, :], gT[:, n, m, :], ys_hi[:, m, :].bitcast(F32),
                                        ALU.subtract).then_inc(s_ylo, 1)

            PER = 9

            def first_sum(n, pair):
                dve.wait_ge(s_omm, n * 2 + pair + 1)
                dve.wait_ge(s_xb, n + 1)
                for e in range(2):
                    t = 2 * pair + e
                    done = nc.vector.scalar_tensor_tensor(out=x1_rows[:, t, :], in0=x1_rows[:, t, :], scalar=2.0,
                                                          in1=bank[6 + pair][:, e * DM:(e + 1) * DM], op0=ALU.mult,
                                                          op1=ALU.add)
                done.then_inc(s_ln, 1)

            def spread(which, rows, tiles):
                for t in tiles:
                    done = nc.vector.bn_stats(stats[:, which, t, :], rows[:, t, :])
                done.then_inc(s_ln, 1)

            def mean_and_variance(which, tiles):
                for t in tiles:
                    done = nc.vector.bn_aggr(moments[:, which, t, :], stats[:, which, t, :])
                done.then_inc(s_ln, 1)

            def add_eps(which, tiles, done_sem):
                lo, hi = tiles[0], tiles[-1] + 1
                nc.vector.tensor_scalar(rstd[:, which, lo:hi], moments[:, which, lo:hi, 1], LN_EPS, None,
                                        ALU.add).then_inc(done_sem, 1)

            def normalise(which, rows, tiles, done_sem):
                for t in tiles:
                    done = nc.vector.tensor_scalar(rows[:, t, :], rows[:, t, :], moments[:, which, t, 0:1],
                                                   rstd[:, which, t:t + 1], ALU.subtract, ALU.mult)
                done.then_inc(done_sem, 1)

            PAIRS = ((0, 1), (2, 3))
            ALL = (0, 1, 2, 3)

            def first_norm(n, pair):
                dve.wait_ge(s_rs1, n * 2 + pair + 1)
                normalise(0, x1_rows, PAIRS[pair], s_x1)

            def second_norm(n):
                dve.wait_ge(s_rs2, n + 1)
                normalise(1, rows_of(gT, n), ALL, s_or)

            def x1_lo(n, pair):
                dve.wait_ge(s_xhi, n * 2 + pair + 1)
                nc.vector.scalar_tensor_tensor(
                    out=x1T[:, n, 1, 2 * pair:2 * pair + 2].rearrange("p s k r -> p (s k r)"),
                    in0=bank[6 + pair][:, :], scalar=X_SCALE,
                    in1=x1T[:, n, 0, 2 * pair:2 * pair + 2].rearrange("p s k r -> p (s k r)"),
                    op0=ALU.mult, op1=ALU.subtract).then_inc(s_xlo, 1)

            def hidden_lo(n, c):
                dve.wait_ge(s_hhi, n * HC + c + 1)
                nc.vector.scalar_tensor_tensor(out=hid[:, c % 3, 1, :], in0=g32[:, c % 2, :],
                                               scalar=hid_scale[:, 0:1], in1=hid[:, c % 3, 0, :], op0=ALU.mult,
                                               op1=ALU.subtract).then_inc(s_hlo, 1)

            def pair_sums(pair):
                return nc.vector.tensor_tensor(fin[:, 2 * pair:2 * pair + 2, :],
                                               bank[pair][:, :].rearrange("p (e d) -> p e d", d=DM),
                                               alpha2_row[:, None, :].broadcast_to([P, 2, DM]), ALU.mult)

            def ffn_scale(n):
                dve.wait_ge(s_f2, n * HC + HC)
                for pair in range(2):
                    pair_sums(pair).then_inc(s_fin, 1)

            def iteration(n, stage_y, stage_a, final, store, base, kept=()):
                link = base
                rows2 = rows_of(gT, n - 1) if final else None
                if store:
                    second_norm(n - 2)
                if stage_y:
                    gate_y(n + 2, 0)
                if stage_a:
                    ys_low(n + 1, 0)
                    ys_low(n + 1, 1)
                hidden_lo(n, 0)
                if stage_y:
                    gate_y(n + 2, 1)
                if final:
                    ffn_scale(n - 1)
                hidden_lo(n, 1)
                if stage_a:
                    first_sum(n + 1, 0)
                    link += 1
                    dve.wait_ge(s_ln, link)
                    spread(0, x1_rows, PAIRS[0])
                    link += 1
                    spread0 = link
                    first_sum(n + 1, 1)
                    link += 1
                    sum1 = link
                    dve.wait_ge(s_ln, spread0)
                hidden_lo(n, 2)
                if stage_a:
                    mean_and_variance(0, PAIRS[0])
                    link += 1
                    moments0 = link
                    dve.wait_ge(s_ln, sum1)
                    spread(0, x1_rows, PAIRS[1])
                    link += 1
                    spread1 = link
                    dve.wait_ge(s_ln, moments0)
                    add_eps(0, PAIRS[0], s_v1)
                if final:
                    dve.wait_ge(s_r2, n)
                    spread(1, rows2, PAIRS[0])
                    link += 1
                hidden_lo(n, 3)
                if stage_a:
                    dve.wait_ge(s_ln, spread1)
                    first_norm(n + 1, 0)
                    mean_and_variance(0, PAIRS[1])
                    link += 1
                    moments1 = link
                if final:
                    spread(1, rows2, PAIRS[1])
                    link += 1
                    spread2 = link
                if stage_a:
                    dve.wait_ge(s_ln, moments1)
                    add_eps(0, PAIRS[1], s_v1)
                if final:
                    dve.wait_ge(s_ln, spread2)
                hidden_lo(n, 4)
                if stage_a:
                    first_norm(n + 1, 1)
                for late in kept[:1]:
                    keep_x(late)
                if final:
                    mean_and_variance(1, ALL)
                    link += 1
                    moments2 = link
                hidden_lo(n, 5)
                if final:
                    dve.wait_ge(s_ln, moments2)
                    add_eps(1, ALL, s_v2)
                hidden_lo(n, 6)
                if stage_a:
                    x1_lo(n + 1, 0)
                    x1_lo(n + 1, 1)
                hidden_lo(n, 7)
                for late in kept[1:]:
                    keep_x(late)
                return link

            def align(n):
                for step in range(n * STEPS, (n + 1) * STEPS):
                    if step > 0:
                        dve.wait_ge(s_shift, step)
                    nc.vector.tensor_copy(hu[0:NS, step, :], hu[0:NS, step + 1, :]).then_inc(s_shift, 1)

            align(0)
            keep_x(GATED - 1)
            for m in range(KD):
                gate_y(0, m)
            align(1)
            keep_x(GATED)
            for m in range(KD):
                ys_low(0, m)
            align(2)
            keep_x(GATED + 1)
            link = 0
            for pair in range(2):
                first_sum(0, pair)
                link += 1
                dve.wait_ge(s_ln, link)
                spread(0, x1_rows, PAIRS[pair])
                link += 1
                dve.wait_ge(s_ln, link)
                mean_and_variance(0, PAIRS[pair])
                link += 1
                dve.wait_ge(s_ln, link)
                add_eps(0, PAIRS[pair], s_v1)
            for pair in range(2):
                first_norm(0, pair)
            for m in range(KD):
                gate_y(1, m)
            dve.wait_ge(s_x1, 2)
            nc.vector.tensor_tensor(rows_of(gT, 0), x1_rows[:, :, :], b2_row[:, None, :].broadcast_to([P, STEPS, DM]),
                                    ALU.add).then_inc(s_x1b, 1)
            for pair in range(2):
                x1_lo(0, pair)
            at = iteration(0, True, True, False, False, link, kept=(GATED + 2, GATED + 3))
            at = iteration(1, True, True, True, False, at, kept=(GATED + 4,))
            with dve.Fori(2, NB - 2) as i:
                iteration(i, True, True, True, True, i * PER + (at - 2 * PER))
            at = iteration(NB - 2, False, True, True, True, at + (NB - 4) * PER)
            at = iteration(NB - 1, False, False, True, True, at)
            second_norm(NB - 2)
            link = at
            last = rows_of(gT, NB - 1)
            dve.wait_ge(s_f2, NB * HC)
            for pair in range(2):
                pair_sums(pair).then_inc(s_fin, 1)
            dve.wait_ge(s_fin, NB * 2)
            nc.vector.tensor_tensor(last[:, 2:4, :], fin[:, 2:4, :], last[:, 2:4, :], ALU.add).then_inc(s_ln, 1)
            dve.wait_ge(s_ln, link + 1)
            spread(1, last, PAIRS[1])
            dve.wait_ge(s_r2, NB)
            spread(1, last, PAIRS[0])
            dve.wait_ge(s_ln, link + 2)
            mean_and_variance(1, PAIRS[1])
            dve.wait_ge(s_ln, link + 3)
            mean_and_variance(1, PAIRS[0])
            dve.wait_ge(s_ln, link + 4)
            add_eps(1, PAIRS[1], s_v2)
            dve.wait_ge(s_ln, link + 5)
            add_eps(1, PAIRS[0], s_v2)
            for done, pair in enumerate((1, 0)):
                dve.wait_ge(s_rs2, NB + done)
                normalise(1, last, PAIRS[pair], s_or)


_INS = ['L0_attn_x', 'L0_attn_W_in', 'L0_attn_b_in', 'L0_attn_W_gate', 'L0_attn_b_gate', 'L0_attn_A', 'L0_attn_Bm',
        'L0_attn_C', 'L0_attn_D', 'L0_attn_W_out', 'L0_attn_b_out', 'L0_ffn_w1', 'L0_ffn_b1', 'L0_ffn_w2', 'L0_ffn_b2']


def kernel(**inputs):
    import numpy as _np
    import concourse.bacc as _bacc
    from concourse import mybir as _mybir
    from concourse.bass_utils import run_bass_kernel_spmd as _run

    nc = _bacc.Bacc("TRN2", target_bir_lowering=False, num_devices=1)
    arrays, args = {}, []
    for name in _INS:
        a = _np.ascontiguousarray(inputs[name])
        arrays[f"in_{name}"] = a
        args.append(nc.dram_tensor(f"in_{name}", a.shape, _mybir.dt.from_np(a.dtype), kind="ExternalInput").ap())
    shape = arrays["in_L0_attn_x"].shape
    args.append(nc.dram_tensor("out_rows", shape, _mybir.dt.float32, kind="ExternalOutput").ap())
    gated_rnn_ffn(nc, *args)
    r = _run(nc, [arrays], core_ids=[0])
    return r.results[0]["out_rows"]
```
